# Optimizing a Trainium2 kernel written in Bass

```python
import numpy as np
import jax
import jax.numpy as jnp

def _softmax(x, axis=-1):
    return jax.nn.softmax(x, axis=axis)

def _gelu(x):
    return jax.nn.gelu(x, approximate=True)

def _silu(x):
    return jax.nn.silu(x)

def _sigmoid(x):
    return jax.nn.sigmoid(x)

def _layernorm(x, axis=-1, eps=1e-05):
    m = jnp.mean(x, axis=axis, keepdims=True)
    v = jnp.var(x, axis=axis, keepdims=True)
    return (x - m) / jnp.sqrt(v + eps)

def _scatter_add(tgt, idx, src, axis=0):
    return tgt.at[idx].add(src)

def _segment_sum(src, seg, n):
    return jax.ops.segment_sum(src, seg, n)
kernel_name = 'mk_gnn_preln_d1_gnn_r64_7ba095'

def setup_inputs(seed: int=0):
    np.random.seed(seed)
    _w = jnp.asarray

    def _rec_inputs():
        import jax
        import jax.numpy as jnp
        _gk = jax.random.key(seed)
        x = -0.0005121 + 1.001 * jax.random.normal(jax.random.fold_in(_gk, 1), (100000, 64), jnp.float32)
        src = jax.random.randint(jax.random.fold_in(_gk, 2), (25000,), 0, 100000, jnp.int32)
        dst = jnp.minimum((100000 * jax.random.uniform(jax.random.fold_in(_gk, 3), (25000,)) ** 2.0).astype(jnp.int32), 99999)
        _o = jnp.argsort(dst, stable=True)
        src = src[_o]
        dst = dst[_o]
        edge_attr_64 = -9.77346e-05 + 0.999888 * jax.random.normal(jax.random.fold_in(_gk, 12), (25000, 64), jnp.float32)
        return (x, src, dst, edge_attr_64)
    x, src, dst, edge_attr_64 = _rec_inputs()

    def _L0_gnn_setup():
        import jax, jax.numpy as jnp
        import numpy as np
        N_NODES = 50000
        N_EDGES = 12500
        D_NODE = 64
        D_EDGE = 64
        D_MSG = 128
        D_EIN = 2 * D_NODE + D_EDGE
        D_NIN = D_MSG + D_NODE

        def _mlp2(x, W1, b1, W2, b2):
            return jax.nn.relu(x @ W1 + b1) @ W2 + b2
        key = jax.random.key(seed)
        ks = jax.random.split(key, 16)
        s = 0.05
        return {'node_states': jax.random.normal(ks[0], (N_NODES, D_NODE), jnp.float32), 'edge_features': jax.random.normal(ks[1], (N_EDGES, D_EDGE), jnp.float32), 'W1_f': jax.random.normal(ks[2], (D_EIN, D_MSG), jnp.float32) * s, 'b1_f': jnp.zeros((D_MSG,), jnp.float32), 'W2_f': jax.random.normal(ks[3], (D_MSG, D_MSG), jnp.float32) * s, 'b2_f': jnp.zeros((D_MSG,), jnp.float32), 'W1_r': jax.random.normal(ks[4], (D_EIN, D_MSG), jnp.float32) * s, 'b1_r': jnp.zeros((D_MSG,), jnp.float32), 'W2_r': jax.random.normal(ks[5], (D_MSG, D_MSG), jnp.float32) * s, 'b2_r': jnp.zeros((D_MSG,), jnp.float32), 'Wn1': jax.random.normal(ks[6], (D_NIN, D_MSG), jnp.float32) * s, 'bn1': jnp.zeros((D_MSG,), jnp.float32), 'Wn2': jax.random.normal(ks[7], (D_MSG, D_NODE), jnp.float32) * s, 'bn2': jnp.zeros((D_NODE,), jnp.float32), 'from_idx': jax.random.randint(ks[8], (N_EDGES,), 0, N_NODES, jnp.int32), 'to_idx': jax.random.randint(ks[9], (N_EDGES,), 0, N_NODES, jnp.int32)}
    _L0_gnn_all = _L0_gnn_setup()
    _L0_gnn_in = {k: v for k, v in _L0_gnn_all.items() if k in ('W1_f', 'b1_f', 'W2_f', 'b2_f', 'W1_r', 'b1_r', 'W2_r', 'b2_r', 'Wn1', 'bn1', 'Wn2', 'bn2')}
    del _L0_gnn_all
    return {'x': x, 'src': src, 'dst': dst, 'edge_attr_64': edge_attr_64, 'L0_gnn_W1_f': _L0_gnn_in['W1_f'], 'L0_gnn_b1_f': _L0_gnn_in['b1_f'], 'L0_gnn_W2_f': _L0_gnn_in['W2_f'], 'L0_gnn_b2_f': _L0_gnn_in['b2_f'], 'L0_gnn_W1_r': _L0_gnn_in['W1_r'], 'L0_gnn_b1_r': _L0_gnn_in['b1_r'], 'L0_gnn_W2_r': _L0_gnn_in['W2_r'], 'L0_gnn_b2_r': _L0_gnn_in['b2_r'], 'L0_gnn_Wn1': _L0_gnn_in['Wn1'], 'L0_gnn_bn1': _L0_gnn_in['bn1'], 'L0_gnn_Wn2': _L0_gnn_in['Wn2'], 'L0_gnn_bn2': _L0_gnn_in['bn2']}

def reference(x, src, dst, edge_attr_64, L0_gnn_W1_f, L0_gnn_b1_f, L0_gnn_W2_f, L0_gnn_b2_f, L0_gnn_W1_r, L0_gnn_b1_r, L0_gnn_W2_r, L0_gnn_b2_r, L0_gnn_Wn1, L0_gnn_bn1, L0_gnn_Wn2, L0_gnn_bn2):
    import jax
    import jax.numpy as jnp

    def _L0_gnn_ref(node_states, edge_features, W1_f, b1_f, W2_f, b2_f, W1_r, b1_r, W2_r, b2_r, Wn1, bn1, Wn2, bn2, from_idx, to_idx):
        import jax, jax.numpy as jnp
        import numpy as np
        N_NODES = 50000
        N_EDGES = 12500
        D_NODE = 64
        D_EDGE = 64
        D_MSG = 128
        D_EIN = 2 * D_NODE + D_EDGE
        D_NIN = D_MSG + D_NODE

        def _mlp2(x, W1, b1, W2, b2):
            return jax.nn.relu(x @ W1 + b1) @ W2 + b2
        n_nodes = node_states.shape[0]
        edge_in_f = jnp.concatenate([node_states[from_idx], node_states[to_idx], edge_features], axis=-1)
        msgs_f = _mlp2(edge_in_f, W1_f, b1_f, W2_f, b2_f)
        agg = jax.ops.segment_sum(msgs_f, to_idx, num_segments=n_nodes)
        edge_in_r = jnp.concatenate([node_states[to_idx], node_states[from_idx], edge_features], axis=-1)
        msgs_r = _mlp2(edge_in_r, W1_r, b1_r, W2_r, b2_r)
        agg = agg + jax.ops.segment_sum(msgs_r, from_idx, num_segments=n_nodes)
        node_in = jnp.concatenate([agg, node_states], axis=-1)
        return node_states + _mlp2(node_in, Wn1, bn1, Wn2, bn2)
    h = jnp.maximum(_layernorm(x, axis=-1), 0.0)
    x = x + _L0_gnn_ref(h, edge_attr_64, L0_gnn_W1_f, L0_gnn_b1_f, L0_gnn_W2_f, L0_gnn_b2_f, L0_gnn_W1_r, L0_gnn_b1_r, L0_gnn_W2_r, L0_gnn_b2_r, L0_gnn_Wn1, L0_gnn_bn1, L0_gnn_Wn2, L0_gnn_bn2, src, dst)
    return x

_drawn_inputs = setup_inputs


def setup_inputs(seed=0):
    import zlib

    import numpy as np

    out = dict(_drawn_inputs(seed))
    spreads = {'L0_gnn_b1_f': (0.0, 0.8),
     'L0_gnn_b2_f': (0.0, 0.8),
     'L0_gnn_b1_r': (0.0, 0.8),
     'L0_gnn_b2_r': (0.0, 0.8),
     'L0_gnn_bn1': (0.0, 0.364),
     'L0_gnn_bn2': (0.0, 0.1)}
    factors = {'edge_attr_64': 4.323,
     'L0_gnn_W1_f': 4.35,
     'L0_gnn_W2_f': 3.348,
     'L0_gnn_W1_r': 4.436,
     'L0_gnn_W2_r': 3.92}
    for name, (base, spread) in spreads.items():
        noise = np.random.default_rng([zlib.crc32(name.encode()), seed]).standard_normal(out[name].shape)
        drawn = base * np.exp(spread * noise) if base else spread * noise
        out[name] = jnp.asarray(drawn.astype(out[name].dtype))
    for name, factor in factors.items():
        out[name] = (out[name] * factor).astype(out[name].dtype)
    return out
```

```python
from contextlib import ExitStack

import concourse.bass as bass
from concourse import mybir

F32 = mybir.dt.float32
I32 = mybir.dt.int32
ALU = mybir.AluOpType
ACT = mybir.ActivationFunctionType
AX = mybir.AxisListType

P = 128
EPS = 1e-5


def gnn_layer(nc, x, src, dst, edge_attr, W1_f, b1_f, W2_f, b2_f, W1_r, b1_r, W2_r, b2_r, Wn1, bn1, Wn2, bn2, out):
    N, D = x.shape
    E = src.shape[0]
    M = W2_f.shape[1]
    assert D == 64 and M == P
    SRC, DST = 0, 1

    JT = 2
    KB = 2 * JT
    NT = -(-E // (P * JT)) * JT
    NB = NT // JT
    PAIRS = NB // 2
    TB = NT // 2
    TAIL = E - (NT - 1) * P
    assert NB % 2 == 0 and 0 < TAIL < P and TB < P

    SPARE = N
    PAD = SPARE + KB * P
    ROWS = -(-(PAD + 2 * P) // P) * P
    ZD = 32
    ZC = ROWS * M // P // ZD
    assert ZC * ZD * P == ROWS * M

    G = 8
    WIN = G * P
    NW = -(-N // WIN)
    WPAIRS = NW // 2
    LASTP = (N - (NW - 1) * WIN) // G
    assert NW % 2 == 0 and N % G == 0

    table = nc.dram_tensor("table", (ROWS, M), F32, kind="Internal").ap()
    numbers = nc.dram_tensor("numbers", (2, NT * P), I32, kind="Internal").ap()
    table_flat = table.rearrange("(p a) m -> p (a m)", p=P)

    with ExitStack() as ctx:
        def sb(name, shape, dt=F32):
            return ctx.enter_context(nc.sbuf_tensor(name, shape, dt))

        def sem(name):
            return ctx.enter_context(nc.semaphore(name))

        def sems(name):
            return [sem(f"{name}{s}") for s in range(2)]

        bank = [ctx.enter_context(nc.psum_tensor(f"bank{b}", [P, 512], F32)) for b in range(8)]

        ident = sb("ident", [P, P])
        earlier = sb("earlier", [P, KB * P])
        spare = sb("spare", [P, KB])
        eps = sb("eps", [P, 1])
        zeros = sb("zeros", [P, ZC])
        w1_ends = sb("w1_ends", [P, 2, M])
        w1_edge = sb("w1_edge", [D, 2, M])
        w2 = sb("w2", [P, 2, M])
        w2t = sb("w2t", [P, 2, M])
        w2n = sb("w2n", [P, 2, M])
        wn1_agg = sb("wn1_agg", [P, M])
        wn1_h = sb("wn1_h", [P, M])
        wn2 = sb("wn2", [P, D])
        b1 = sb("b1", [P, 2])
        b2 = sb("b2", [P, 2])
        b2_wide = sb("b2_wide", [P, 2, P])
        b2n = sb("b2n", [P, KB, M])
        bn1_col = sb("bn1_col", [P, 1])
        bn2_rows = sb("bn2_rows", [P, G, D])

        ends_int = sb("ends_int", [TB, 2, 2, P], I32)
        ends_row = sb("ends_row", [TB, 2, 2, P])
        ends_col = sb("ends_col", [P, NT, 2])

        def two(name, shape, dt=F32):
            return [sb(f"{name}{s}", [P] + shape, dt) for s in range(2)]

        edge_in = two("edge_in", [JT, D])
        others = two("others", [JT, 2, P], I32)
        ids = two("ids", [KB])
        gather_at = two("gather_at", [KB], I32)
        got = two("got", [KB, D])
        sums = two("sums", [KB])
        centred = two("centred", [KB, D])
        squares = two("squares", [KB, D])
        var = two("var", [KB])
        std = two("std", [KB])
        rstd = two("rstd", [KB])
        h_ends = two("h_ends", [KB, D])
        turned = two("turned", [JT * P])
        turned_edge = [sb(f"turned_edge{s}", [D, JT * P]) for s in range(2)]
        hidden = two("hidden", [2, JT * P])
        message = two("message", [KB, M])
        same = two("same", [KB, KB * P])
        junk = two("junk", [KB, KB * P])
        before = two("before", [KB])
        to_spare = two("to_spare", [KB])
        moved = two("moved", [KB])
        scatter_at = two("scatter_at", [KB], I32)
        to_send = two("to_send", [KB, M])

        nx = two("nx", [G, D])
        ntab = two("ntab", [G, M])
        nsums = two("nsums", [G])
        ncentred = two("ncentred", [G, D])
        nsquares = two("nsquares", [G, D])
        nvar = two("nvar", [G])
        nstd = two("nstd", [G])
        nrstd = two("nrstd", [G])
        nh = two("nh", [G, D])
        nxb = two("nxb", [G, D])
        nxh = two("nxh", [G, D])
        nturned = two("nturned", [G // 2 * P])
        nhidden = two("nhidden", [G * P])
        nout = two("nout", [G, D])

        s_params = sem("params_in")
        s_padded = sem("pad_numbers_written")
        s_ends = sem("ends_in")
        s_numbers = sem("numbers_stored")
        s_zeros = sem("zeros_made")
        s_table0 = sem("table_zeroed")
        s_filled = sem("constants_filled")
        s_const = sem("constants_ready")
        s_rowf = sem("ends_as_float")
        s_b2wide = sem("b2_widened")
        s_setup_pe = sem("setup_products")
        s_setup_ev = sem("setup_copied")

        s_edge_in = sems("edge_in_")
        s_others = sems("others_in_")
        s_gat = sems("gather_at_ready")
        s_got = sems("rows_gathered")
        s_sums = sems("sums_ready")
        s_centred = sems("centred_ready")
        s_squared = sems("squares_ready")
        s_var = sems("var_ready")
        s_std = sems("std_ready")
        s_rstd = sems("rstd_ready")
        s_h = sems("h_ends_ready")
        s_turn = sems("transposed")
        s_turned = sems("turned_ready")
        s_l1 = sems("layer1_done")
        s_hidden = sems("hidden_ready")
        s_l2 = sems("layer2_done")
        s_message = sems("message_ready")
        s_ids = sems("ids_ready")
        s_same = sems("same_ready")
        s_before = sems("before_counted")
        s_tospare = sems("to_spare_ready")
        s_moved = sems("moved_ready")
        s_sat = sems("scatter_at_ready")
        s_joined = sems("joined")
        s_send = sems("to_send_ready")
        s_added = sems("rows_added")

        s_gathers_begun = sem("gathers_begun")
        s_scatters_begun = sem("scatters_begun")

        n_x = sems("n_x_in")
        n_tab = sems("n_table_in")
        n_sums = sems("n_sums_ready")
        n_centred = sems("n_centred_ready")
        n_squared = sems("n_squares_ready")
        n_var = sems("n_var_ready")
        n_std = sems("n_std_ready")
        n_rstd = sems("n_rstd_ready")
        n_h = sems("n_h_ready")
        n_xb = sems("n_x_plus_bias")
        n_xh = sems("n_x_plus_h")
        n_turn = sems("n_transposed")
        n_turned = sems("n_turned_ready")
        n_l1 = sems("n_layer1_done")
        n_hidden = sems("n_hidden_ready")
        n_l2 = sems("n_layer2_done")
        n_out = sems("n_out_ready")
        n_stored = sems("n_stored")

        N_PARAMS = 17

        block = ctx.enter_context(nc.Block())

        def pairs(eng, count, body):
            body(0)
            with eng.Fori(1, count - 1) as i:
                body(eng.snap(i))
            body(count - 1)

        def first(i):
            return isinstance(i, int) and i == 0

        @block.sync
        def _(sp):
            def param(to, of):
                sp.dma_start(to, of).then_inc(s_params, 16)

            sp.wait_ge(s_padded, 2)
            for end, a in ((SRC, src), (DST, dst)):
                full = TB * P
                rest = (TB - 1) * P
                sp.dma_start(ends_int[:, end, 0, :], a[0:full].rearrange("(t p) -> t p", p=P)).then_inc(s_ends, 16)
                sp.dma_start(ends_int[0:TB - 1, end, 1, :],
                             a[full:full + rest].rearrange("(t p) -> t p", p=P)).then_inc(s_ends, 16)
                sp.dma_start(ends_int[TB - 1:TB, end, 1, 0:TAIL],
                             a[full + rest:E].rearrange("(t p) -> t p", t=1)).then_inc(s_ends, 16)
            param(w2[:, 0, :], W2_r)
            param(w2[:, 1, :], W2_f)
            param(wn1_agg[:, :], Wn1[0:M, :])
            param(b2[:, 0:1], b2_r.rearrange("(p a) -> p a", a=1))
            param(b2[:, 1:2], b2_f.rearrange("(p a) -> p a", a=1))
            param(w1_ends[:, 1, :], W1_f[0:2 * D, :])
            param(w1_ends[0:D, 0, :], W1_r[D:2 * D, :])
            param(w1_ends[D:2 * D, 0, :], W1_r[0:D, :])
            param(w1_edge[:, 0, :], W1_r[2 * D:3 * D, :])
            param(w1_edge[:, 1, :], W1_f[2 * D:3 * D, :])
            param(b1[:, 0:1], b1_r.rearrange("(p a) -> p a", a=1))
            param(b1[:, 1:2], b1_f.rearrange("(p a) -> p a", a=1))
            param(wn1_h[0:D, :], Wn1[M:M + D, :])
            param(wn1_h[D:2 * D, :], Wn1[M:M + D, :])
            param(wn2[:, :], Wn2)
            sp.wait_ge(s_ends, 6 * 16)
            for end in (SRC, DST):
                sp.dma_start(numbers[end, :].rearrange("(b t p) -> t b p", b=2, p=P),
                             ends_int[:, end, :, :]).then_inc(s_numbers, 16)
            sp.wait_ge(s_numbers, 32)

            def load(i, s):
                last = isinstance(i, int) and i == PAIRS - 1 and s == 1
                first_edge = (2 * i + s) * (JT * P)
                if not first(i):
                    sp.wait_ge(s_turn[s], i)
                    sp.wait_ge(s_same[s], i)
                if last:
                    sp.dma_start(edge_in[s][:, 0, :],
                                 edge_attr[first_edge:first_edge + P, :]).then_inc(s_edge_in[s], 16)
                    sp.dma_start(edge_in[s][0:TAIL, 1, :], edge_attr[first_edge + P:E, :]).then_inc(s_edge_in[s], 16)
                else:
                    sp.dma_start(edge_in[s][:, :, :], edge_attr[bass.ds(first_edge, JT * P), :]
                                 .rearrange("(j p) d -> p j d", p=P)).then_inc(s_edge_in[s], 16)
                for end in (SRC, DST):
                    sp.dma_start(others[s][:, :, end, :],
                                 numbers[end:end + 1, bass.ds(first_edge, JT * P)]
                                 .rearrange("a (j p) -> a j p", p=P).to_broadcast([P, JT, P])
                                 ).then_inc(s_others[s], 16)

            pairs(sp, PAIRS, lambda i: [load(i, s) for s in range(2)])

            def node_rows(a, i, s):
                return a[bass.ds((2 * i + s) * WIN, WIN), :].rearrange("(p g) d -> p (g d)", g=G)

            def is_last(i, s):
                return isinstance(i, int) and i == WPAIRS - 1 and s == 1

            def last_rows(a):
                return a[(NW - 1) * WIN:N, :].rearrange("(p g) d -> p (g d)", g=G)

            def load_x(i, s):
                if not first(i):
                    sp.wait_ge(n_centred[s], i)
                    sp.wait_ge(n_xb[s], i)
                to = nx[s][:, :, :].rearrange("p g d -> p (g d)")
                if is_last(i, s):
                    sp.dma_start(to[0:LASTP, :], last_rows(x)).then_inc(n_x[s], 16)
                else:
                    sp.dma_start(to, node_rows(x, i, s)).then_inc(n_x[s], 16)

            def load_table(i, s):
                if not first(i):
                    sp.wait_ge(n_l1[s], 2 * i)
                to = ntab[s][:, :, :].rearrange("p g d -> p (g d)")
                if is_last(i, s):
                    sp.dma_start(to[0:LASTP, :], last_rows(table[0:N, :])).then_inc(n_tab[s], 16)
                else:
                    sp.dma_start(to, node_rows(table, i, s)).then_inc(n_tab[s], 16)

            def store(i, s):
                sp.wait_ge(n_out[s], i + 1)
                of = nout[s][:, :, :].rearrange("p g d -> p (g d)")
                if is_last(i, s):
                    sp.dma_start(last_rows(out), of[0:LASTP, :]).then_inc(n_stored[s], 16)
                else:
                    sp.dma_start(node_rows(out, i, s), of).then_inc(n_stored[s], 16)

            for s in range(2):
                load_x(0, s)
            for s in range(2):
                sp.wait_ge(s_added[s], 16 * KB * PAIRS)
            for s in range(2):
                load_table(0, s)

            def window_pair(i):
                for s in range(2):
                    load_x(i + 1, s)
                    load_table(i + 1, s)
                    store(i, s)

            window_pair(0)
            with sp.Fori(1, WPAIRS - 2) as i:
                window_pair(sp.snap(i))
            window_pair(WPAIRS - 2)
            for s in range(2):
                store(WPAIRS - 1, s)
            for s in range(2):
                sp.wait_ge(n_stored[s], 16 * WPAIRS)

        @block.gpsimd
        def _(pool):
            for end in (SRC, DST):
                pool.iota(ends_int[:, end, :, :], pattern=[[0, 2], [1, P]], base=PAD + end * P,
                          channel_multiplier=0).then_inc(s_padded, 1)
            pool.iota(spare[:, :], pattern=[[P, KB]], base=SPARE, channel_multiplier=1,
                      allow_small_or_imprecise_dtypes=True).then_inc(s_const, 1)
            pool.memset(ident[:, :], 0.0).then_inc(s_filled, 1)
            pool.memset(earlier[:, :], 1.0).then_inc(s_filled, 1)
            pool.wait_ge(s_filled, 2)
            pool.affine_select(out=ident[:, :], in_=ident[:, :], compare_op=ALU.not_equal, fill=1.0, base=0,
                               pattern=[[-1, P]], channel_multiplier=1).then_inc(s_const, 1)
            tail = earlier[:, (KB - 1) * P:]
            pool.affine_select(out=tail, in_=tail, compare_op=ALU.is_gt, fill=0.0, base=0,
                               pattern=[[-1, P]], channel_multiplier=1).then_inc(s_const, 1)

            def gather(i, s):
                pool.wait_ge(s_gat[s], i + 1)
                if not first(i):
                    pool.wait_ge(s_centred[s], i)
                pool.sem_inc(s_gathers_begun, 1)
                for k in range(KB):
                    pool.indirect_dma_start(got[s][:, k, :], None, x,
                                            bass.IndirectOffsetOnAxis(ap=gather_at[s][:, k:k + 1], axis=0)
                                            ).then_inc(s_got[s], 16)

            def scatter(i, s):
                pool.wait_ge(s_sat[s], i + 1)
                pool.wait_ge(s_send[s], i + 1)
                if s == 1:
                    pool.wait_ge(s_added[0], 16 * KB * (i + 1))
                elif not first(i):
                    pool.wait_ge(s_added[1], 16 * KB * i)
                else:
                    pool.wait_ge(s_table0, 16 * ZD)
                pool.sem_inc(s_scatters_begun, 1)
                for k in range(KB):
                    pool.indirect_dma_start(table, bass.IndirectOffsetOnAxis(ap=scatter_at[s][:, k:k + 1], axis=0),
                                            to_send[s][:, k, :], None, compute_op=ALU.add).then_inc(s_added[s], 16)

            gather(0, 0)
            gather(0, 1)

            def batch_pair(i):
                for s in range(2):
                    scatter(i, s)
                    gather(i + 1, s)

            batch_pair(0)
            with pool.Fori(1, PAIRS - 1) as i:
                batch_pair(pool.snap(i))
            for s in range(2):
                scatter(PAIRS - 1, s)

            def sum_x(i, s):
                pool.wait_ge(n_x[s], 16 * (i + 1))
                if first(i) and s == 0:
                    pool.wait_ge(s_params, 16 * N_PARAMS)
                pool.tensor_tensor(nxb[s][:, :, :], nx[s][:, :, :], bn2_rows[:, :, :], ALU.add).then_inc(n_xb[s], 1)
                pool.wait_ge(n_xb[s], i + 1)
                pool.wait_ge(n_h[s], i + 1)
                if not first(i):
                    pool.wait_ge(n_out[s], i)
                pool.tensor_tensor(nxh[s][:, :, :], nxb[s][:, :, :], nh[s][:, :, :], ALU.add).then_inc(n_xh[s], 1)

            pairs(pool, WPAIRS, lambda i: [sum_x(i, s) for s in range(2)])

        @block.scalar
        def _(act):
            act.dma_start(bn1_col[:, :], bn1.rearrange("(p a) -> p a", a=1)).then_inc(s_params, 16)
            act.dma_start(bn2_rows[:, :, :], bn2.rearrange("(a b d) -> a b d", a=1, b=1)
                          .to_broadcast([P, G, D])).then_inc(s_params, 16)
            act.wait_ge(s_zeros, 1)
            for z in range(ZD):
                act.dma_start(table_flat[:, z * ZC:(z + 1) * ZC],
                              zeros[:, :]).then_inc(s_table0, 16)

            def square(i, s):
                act.wait_ge(s_centred[s], i + 1)
                if not first(i):
                    act.wait_ge(s_var[s], i)
                act.activation(squares[s][:, :, :], centred[s][:, :, :], ACT.Square,
                               scale=D ** -0.5).then_inc(s_squared[s], 1)

            def root(i, s):
                act.wait_ge(s_var[s], i + 1)
                act.activation(std[s][:, :], var[s][:, :], ACT.Sqrt, bias=eps[:, 0:1]).then_inc(s_std[s], 1)

            def copy_turned(i, s):
                act.wait_ge(s_turn[s], i + 1)
                if not first(i):
                    act.wait_ge(s_l1[s], i)
                act.copy(turned[s][:, :], bank[s][:, 0:JT * P]).then_inc(s_turned[s], 1)
                act.copy(turned_edge[s][:, :], bank[s][0:D, JT * P:2 * JT * P]).then_inc(s_turned[s], 1)

            def relu(i, s):
                act.wait_ge(s_l1[s], i + 1)
                if not first(i):
                    act.wait_ge(s_l2[s], i)
                for end in (SRC, DST):
                    act.activation(hidden[s][:, end, :], bank[2 + s][:, end * JT * P:(end + 1) * JT * P], ACT.Relu,
                                   bias=b1[:, end:end + 1]).then_inc(s_hidden[s], 1)

            def copy_sums(i, s):
                act.wait_ge(s_joined[s], i + 1)
                if not first(i):
                    act.wait_ge(s_added[s], 16 * KB * i)
                act.copy(to_send[s][:, :, :].rearrange("p k m -> p (k m)"), bank[6 + s][:, :]).then_inc(s_send[s], 1)

            def batch(i, s):
                square(i, s)
                root(i, s)
                copy_turned(i, s)
                relu(i, s)
                if s == 1:
                    copy_sums(i, 0)
                elif not first(i):
                    copy_sums(i - 1, 1)

            act.wait_ge(s_params, 16 * N_PARAMS)
            pairs(act, PAIRS, lambda i: [batch(i, s) for s in range(2)])
            copy_sums(PAIRS - 1, 1)

            def window(i, s):
                act.wait_ge(n_centred[s], i + 1)
                if not first(i):
                    act.wait_ge(n_var[s], i)
                act.activation(nsquares[s][:, :, :], ncentred[s][:, :, :], ACT.Square,
                               scale=D ** -0.5).then_inc(n_squared[s], 1)
                act.wait_ge(n_var[s], i + 1)
                act.activation(nstd[s][:, :], nvar[s][:, :], ACT.Sqrt, bias=eps[:, 0:1]).then_inc(n_std[s], 1)
                act.wait_ge(n_turn[s], i + 1)
                act.copy(nturned[s][:, :], bank[s][:, :]).then_inc(n_turned[s], 1)
                for half in range(2):
                    act.wait_ge(n_l1[s], 2 * i + 1 + half)
                    if not first(i):
                        act.wait_ge(n_l2[s], i)
                    act.activation(nhidden[s][:, half * 512:half * 512 + 512], bank[2 + 2 * s + half][:, :], ACT.Relu,
                                   bias=bn1_col[:, 0:1]).then_inc(n_hidden[s], 1)

            pairs(act, WPAIRS, lambda i: [window(i, s) for s in range(2)])

        @block.tensor
        def _(pe):
            pe.wait_ge(s_const, 3)
            pe.wait_ge(s_rowf, 1)
            for end in (SRC, DST):
                for b in range(2):
                    c = (2 * end + b) * TB
                    last = pe.transpose(bank[0][:, c:c + TB], ends_row[:, end, b, :], ident[0:TB, 0:TB])
            last.then_inc(s_setup_pe, 1)
            pe.wait_ge(s_params, 16 * N_PARAMS)
            for end in (SRC, DST):
                last = pe.transpose(bank[1][:, end * M:(end + 1) * M], w2[:, end, :], ident[:, :])
            last.then_inc(s_setup_pe, 1)
            pe.wait_ge(s_setup_ev, 3)
            pe.wait_ge(s_b2wide, 2)
            for end in (SRC, DST):
                pe.matmul(bank[2][:, end * M:(end + 1) * M], w2t[:, end, :], wn1_agg[:, :], start=True, stop=True)
            for end in (SRC, DST):
                last = pe.matmul(bank[2][:, (2 + end) * M:(3 + end) * M], b2_wide[:, end, :], wn1_agg[:, :],
                                 start=True, stop=True)
            last.then_inc(s_setup_pe, 1)
            pe.wait_ge(s_setup_ev, 6)

            def turn(i, s):
                if not first(i):
                    pe.wait_ge(s_turned[s], 2 * i)
                if isinstance(i, int) and i == PAIRS - 1 and s == 1:
                    pe.wait_ge(s_edge_in[s], 16 * (i + 2))
                else:
                    pe.wait_ge(s_edge_in[s], 16 * (i + 1))
                pe.wait_ge(s_h[s], i + 1)
                for j in range(JT):
                    pe.transpose(bank[s][:, j * P:(j + 1) * P],
                                 h_ends[s][:, 2 * j:2 * j + 2, :].rearrange("p k d -> p (k d)"), ident[:, :])
                for j in range(JT):
                    last = pe.transpose(bank[s][0:D, (JT + j) * P:(JT + j + 1) * P], edge_in[s][:, j, :], ident[:, :])
                last.then_inc(s_turn[s], 1)

            def layer1(i, s):
                pe.wait_ge(s_turned[s], 2 * (i + 1))
                if not first(i):
                    pe.wait_ge(s_hidden[s], 2 * i)
                for end in (SRC, DST):
                    c = end * JT * P
                    pe.matmul(bank[2 + s][:, c:c + JT * P], w1_ends[:, end, :], turned[s][:, 0:JT * P],
                              start=True, stop=False)
                    last = pe.matmul(bank[2 + s][:, c:c + JT * P], w1_edge[:, end, :], turned_edge[s][:, :],
                                     start=False, stop=True)
                last.then_inc(s_l1[s], 1)

            def layer2(i, s):
                if not first(i):
                    pe.wait_ge(s_message[s], i)
                for end in (SRC, DST):
                    pe.wait_ge(s_hidden[s], 2 * i + 1 + end)
                    for j in range(JT):
                        k = 2 * j + end
                        last = pe.matmul(bank[4 + s][:, k * M:(k + 1) * M], hidden[s][:, end, j * P:(j + 1) * P],
                                         w2n[:, end, :], start=True, stop=True)
                last.then_inc(s_l2[s], 1)

            def join(i, s):
                pe.wait_ge(s_message[s], i + 1)
                pe.wait_ge(s_same[s], i + 1)
                if not first(i):
                    pe.wait_ge(s_send[s], i)
                for k in range(KB):
                    for o in range(KB):
                        last = pe.matmul(bank[6 + s][:, k * M:(k + 1) * M], same[s][:, o, k * P:(k + 1) * P],
                                         message[s][:, o, :], start=(o == 0), stop=(o == KB - 1))
                last.then_inc(s_joined[s], 1)

            def batch(i, s):
                turn(i, s)
                layer1(i, s)
                layer2(i, s)
                if s == 1:
                    join(i, 0)
                elif not first(i):
                    join(i - 1, 1)

            pairs(pe, PAIRS, lambda i: [batch(i, s) for s in range(2)])
            join(PAIRS - 1, 1)

            for s in range(2):
                pe.wait_ge(s_send[s], PAIRS)
                pe.wait_ge(s_message[s], PAIRS)

            def turn_nodes(i, s):
                pe.wait_ge(n_h[s], i + 1)
                if not first(i):
                    pe.wait_ge(n_turned[s], i)
                for q in range(G // 2):
                    last = pe.transpose(bank[s][:, q * P:(q + 1) * P],
                                        nh[s][:, 2 * q:2 * q + 2, :].rearrange("p g d -> p (g d)"), ident[:, :])
                last.then_inc(n_turn[s], 1)

            def layer1_nodes(i, s):
                pe.wait_ge(n_tab[s], 16 * (i + 1))
                pe.wait_ge(n_turned[s], i + 1)
                if not first(i):
                    pe.wait_ge(n_hidden[s], 2 * i)
                for odd in range(2):
                    for q in range(G // 2):
                        pe.matmul(bank[2 + 2 * s + odd][:, q * P:(q + 1) * P], ntab[s][:, 2 * q + odd, :], ident[:, :],
                                  start=(q == 0), stop=False, is_transpose=True)
                for odd in range(2):
                    pe.matmul(bank[2 + 2 * s + odd][:, :], wn1_h[odd * D:(odd + 1) * D, :],
                              nturned[s][odd * D:(odd + 1) * D, :], start=False, stop=True).then_inc(n_l1[s], 1)

            def layer2_nodes(i, s):
                if not first(i):
                    pe.wait_ge(n_out[s], i)
                for odd in range(2):
                    pe.wait_ge(n_hidden[s], 2 * i + 1 + odd)
                    for q in range(G // 2):
                        g, c = 2 * q + odd, (odd * (G // 2) + q) * P
                        last = pe.matmul(bank[6 + s][:, g * D:(g + 1) * D], nhidden[s][:, c:c + P], wn2[:, :],
                                         start=True, stop=True)
                last.then_inc(n_l2[s], 1)

            def window(i, s):
                turn_nodes(i, s)
                if s == 1:
                    layer2_nodes(i, 0)
                elif not first(i):
                    layer2_nodes(i - 1, 1)
                layer1_nodes(i, s)

            pairs(pe, WPAIRS, lambda i: [window(i, s) for s in range(2)])
            layer2_nodes(WPAIRS - 1, 1)

        @block.vector
        def _(dve):
            dve.memset(zeros[:, :], 0.0).then_inc(s_zeros, 1)
            dve.memset(eps[:, :], EPS).then_inc(s_const, 1)
            dve.wait_ge(s_ends, 6 * 16)
            dve.tensor_copy(ends_row[:, :, :, :], ends_int[:, :, :, :]).then_inc(s_rowf, 1)
            dve.wait_ge(s_setup_pe, 1)
            for end in (SRC, DST):
                dve.tensor_copy(ends_col[:, :, end], bank[0][:, 2 * end * TB:(2 * end + 2) * TB]
                                ).then_inc(s_setup_ev, 1)
            dve.wait_ge(s_params, 16 * N_PARAMS)
            for end in (SRC, DST):
                dve.tensor_copy(b2_wide[:, end, :], b2[:, end:end + 1].to_broadcast([P, P])).then_inc(s_b2wide, 1)
            dve.wait_ge(s_setup_pe, 2)
            dve.tensor_copy(w2t[:, :, :].rearrange("p a m -> p (a m)"), bank[1][:, 0:2 * M]).then_inc(s_setup_ev, 1)
            dve.wait_ge(s_setup_pe, 3)
            dve.tensor_copy(w2n[:, :, :].rearrange("p a m -> p (a m)"), bank[2][:, 0:2 * M]).then_inc(s_setup_ev, 1)
            for j in range(JT):
                dve.tensor_copy(b2n[:, 2 * j:2 * j + 2, :].rearrange("p a m -> p (a m)"),
                                bank[2][:, 2 * M:4 * M]).then_inc(s_setup_ev, 1)
            dve.wait_ge(s_setup_ev, 6)
            dve.wait_ge(s_const, 4)

            ends = ends_col[:, :, :].rearrange("p t e -> p (t e)")

            def gather_rows(i, s):
                if not first(i):
                    dve.wait_ge(s_got[s], 16 * KB * i)
                dve.tensor_scalar(gather_at[s][:, :], ends[:, bass.ds((2 * i + s) * KB, KB)], float(N - 1), None,
                                  ALU.min).then_inc(s_gat[s], 1)

            def centre(i, s):
                dve.wait_ge(s_got[s], 16 * KB * (i + 1))
                dve.tensor_reduce(sums[s][:, :], got[s][:, :, :], AX.X, ALU.add).then_inc(s_sums[s], 1)
                dve.wait_ge(s_sums[s], i + 1)
                dve.scalar_tensor_tensor(out=centred[s][:, :, :], in0=sums[s][:, :].to_broadcast([P, KB, D]),
                                         scalar=-1.0 / D, in1=got[s][:, :, :], op0=ALU.mult, op1=ALU.add
                                         ).then_inc(s_centred[s], 1)

            def match(i, s):
                if not first(i):
                    dve.wait_ge(s_sat[s], i)
                dve.tensor_copy(ids[s][:, :], ends[:, bass.ds((2 * i + s) * KB, KB)]).then_inc(s_ids[s], 1)
                dve.wait_ge(s_ids[s], i + 1)
                dve.wait_ge(s_others[s], 32 * (i + 1))
                if not first(i):
                    dve.wait_ge(s_joined[s], i)
                row = others[s][:, :, :, :].rearrange("p j e q -> p (j e q)")
                for o in range(KB):
                    last = dve.tensor_scalar(same[s][:, o, :], row, ids[s][:, o:o + 1], None, ALU.is_equal)
                last.then_inc(s_same[s], 1)

            def variance(i, s):
                dve.wait_ge(s_squared[s], i + 1)
                dve.tensor_reduce(var[s][:, :], squares[s][:, :, :], AX.X, ALU.add).then_inc(s_var[s], 1)

            def targets(i, s):
                dve.wait_ge(s_same[s], i + 1)
                for k in range(KB):
                    w = (k + 1) * P
                    last = dve.tensor_tensor_reduce(junk[s][:, k, 0:w], same[s][:, k, 0:w], earlier[:, KB * P - w:],
                                                    1.0, 0.0, ALU.mult, ALU.add, before[s][:, k:k + 1])
                last.then_inc(s_before[s], 1)
                dve.tensor_tensor(to_spare[s][:, :], spare[:, :], ids[s][:, :], ALU.subtract).then_inc(s_tospare[s], 1)
                dve.wait_ge(s_before[s], i + 1)
                dve.wait_ge(s_tospare[s], i + 1)
                dve.scalar_tensor_tensor(out=moved[s][:, :], in0=before[s][:, :], scalar=1.0, in1=to_spare[s][:, :],
                                         op0=ALU.min, op1=ALU.mult).then_inc(s_moved[s], 1)
                dve.wait_ge(s_moved[s], i + 1)
                if not first(i):
                    dve.wait_ge(s_added[s], 16 * KB * i)
                dve.tensor_tensor(scatter_at[s][:, :], moved[s][:, :], ids[s][:, :], ALU.add).then_inc(s_sat[s], 1)

            def messages(i, s):
                dve.wait_ge(s_l2[s], i + 1)
                if not first(i):
                    dve.wait_ge(s_joined[s], i)
                dve.tensor_tensor(message[s][:, :, :].rearrange("p k m -> p (k m)"), bank[4 + s][:, :],
                                  b2n[:, :, :].rearrange("p k m -> p (k m)"), ALU.add).then_inc(s_message[s], 1)

            def normal(i, s):
                dve.wait_ge(s_std[s], i + 1)
                dve.reciprocal(rstd[s][:, :], std[s][:, :]).then_inc(s_rstd[s], 1)
                dve.wait_ge(s_rstd[s], i + 1)
                if not first(i):
                    dve.wait_ge(s_turn[s], i)
                dve.scalar_tensor_tensor(out=h_ends[s][:, :, :], in0=centred[s][:, :, :], scalar=0.0,
                                         in1=rstd[s][:, :].to_broadcast([P, KB, D]), op0=ALU.max, op1=ALU.mult
                                         ).then_inc(s_h[s], 1)

            def batch(i, s):
                centre(i, s)
                if not (isinstance(i, int) and i == PAIRS - 1):
                    gather_rows(i + 1, s)
                match(i, s)
                variance(i, s)
                targets(i, s)
                if s == 1:
                    messages(i, 0)
                elif not first(i):
                    messages(i - 1, 1)
                normal(i, s)

            for s in range(2):
                gather_rows(0, s)
            pairs(dve, PAIRS, lambda i: [batch(i, s) for s in range(2)])
            messages(PAIRS - 1, 1)

            def centre_nodes(i, s):
                dve.wait_ge(n_x[s], 16 * (i + 1))
                dve.tensor_reduce(nsums[s][:, :], nx[s][:, :, :], AX.X, ALU.add).then_inc(n_sums[s], 1)
                dve.wait_ge(n_sums[s], i + 1)
                dve.scalar_tensor_tensor(out=ncentred[s][:, :, :], in0=nsums[s][:, :].to_broadcast([P, G, D]),
                                         scalar=-1.0 / D, in1=nx[s][:, :, :], op0=ALU.mult, op1=ALU.add
                                         ).then_inc(n_centred[s], 1)

            def output(i, s):
                dve.wait_ge(n_l2[s], i + 1)
                dve.wait_ge(n_xh[s], i + 1)
                if not first(i):
                    dve.wait_ge(n_stored[s], 16 * i)
                dve.tensor_tensor(nout[s][:, :, :].rearrange("p g d -> p (g d)"), bank[6 + s][:, :],
                                  nxh[s][:, :, :].rearrange("p g d -> p (g d)"), ALU.add).then_inc(n_out[s], 1)

            def normal_nodes(i, s):
                dve.wait_ge(n_squared[s], i + 1)
                dve.tensor_reduce(nvar[s][:, :], nsquares[s][:, :, :], AX.X, ALU.add).then_inc(n_var[s], 1)
                dve.wait_ge(n_std[s], i + 1)
                dve.reciprocal(nrstd[s][:, :], nstd[s][:, :]).then_inc(n_rstd[s], 1)
                dve.wait_ge(n_rstd[s], i + 1)
                if not first(i):
                    dve.wait_ge(n_turn[s], i)
                    dve.wait_ge(n_xh[s], i)
                dve.scalar_tensor_tensor(out=nh[s][:, :, :], in0=ncentred[s][:, :, :], scalar=0.0,
                                         in1=nrstd[s][:, :].to_broadcast([P, G, D]), op0=ALU.max, op1=ALU.mult
                                         ).then_inc(n_h[s], 1)

            def window(i, s):
                centre_nodes(i, s)
                if s == 1:
                    normal_nodes(i, s)
                    output(i, 0)
                else:
                    normal_nodes(i, s)
                    if not first(i):
                        output(i - 1, 1)

            pairs(dve, WPAIRS, lambda i: [window(i, s) for s in range(2)])
            output(WPAIRS - 1, 1)


_INS = ['x', 'src', 'dst', 'edge_attr_64', 'L0_gnn_W1_f', 'L0_gnn_b1_f', 'L0_gnn_W2_f', 'L0_gnn_b2_f',
        'L0_gnn_W1_r', 'L0_gnn_b1_r', 'L0_gnn_W2_r', 'L0_gnn_b2_r', 'L0_gnn_Wn1', 'L0_gnn_bn1', 'L0_gnn_Wn2',
        'L0_gnn_bn2']


def kernel(**inputs):
    import numpy as _np
    import concourse.bacc as _bacc
    from concourse import mybir as _mybir
    from concourse.bass_utils import run_bass_kernel_spmd as _run

    nc = _bacc.Bacc("TRN2", target_bir_lowering=False, num_devices=1)
    arrays, args = {}, []
    for name in _INS:
        a = _np.ascontiguousarray(inputs[name])
        arrays[f"in_{name}"] = a
        args.append(nc.dram_tensor(f"in_{name}", a.shape, _mybir.dt.from_np(a.dtype), kind="ExternalInput").ap())
    out = nc.dram_tensor("out_x", inputs["x"].shape, _mybir.dt.float32, kind="ExternalOutput").ap()
    gnn_layer(nc, *args, out)
    r = _run(nc, [arrays], core_ids=[0])
    return r.results[0]["out_x"]
```

```python
from contextlib import ExitStack

import concourse.bass as bass
from concourse import mybir

F32 = mybir.dt.float32
I32 = mybir.dt.int32
ALU = mybir.AluOpType
ACT = mybir.ActivationFunctionType
AX = mybir.AxisListType

P = 128
EPS = 1e-5


class Walk:

    def __init__(self, count, step, uses=None, ring=1, turn=None):
        self.count, self.step, self.uses, self.ring_size, self.turn = count, step, uses, ring, turn

    def there(self, k):
        return self.uses is not None or 0 <= self.step + k < self.count

    def at(self, k):
        n = self.step + k
        return (n // 2 if self.uses is None else self.uses + n // 2), n % 2

    def ring(self, k):
        n = self.step + k
        return (n // self.ring_size if self.turn is None else self.turn + n // self.ring_size), n % self.ring_size

    def do(self, stage, k=0):
        if self.there(k):
            stage(*self.at(k))


def walk(eng, count, unroll, ahead, behind, body):
    assert unroll % 2 == 0 and behind <= unroll
    loops = (count - ahead) // unroll
    for n in range(unroll):
        body(Walk(count, n, ring=unroll))
    with eng.Fori(1, loops) as turn:
        uses = eng.snap(turn * (unroll // 2))
        for n in range(unroll):
            body(Walk(count, n, uses, unroll, turn))
    for n in range(loops * unroll, count + behind):
        body(Walk(count, n, ring=unroll))


def gnn_layer(nc, x, src, dst, edge_attr, W1_f, b1_f, W2_f, b2_f, W1_r, b1_r, W2_r, b2_r, Wn1, bn1, Wn2, bn2, out):
    N, D = x.shape
    E = src.shape[0]
    M = W2_f.shape[1]
    assert D == 64 and M == P
    SRC, DST = 0, 1

    JT = 2
    KB = 2 * JT
    NT = -(-E // (P * JT)) * JT
    NB = NT // JT
    PAIRS = NB // 2
    TB = NT // 2
    TAIL = E - (NT - 1) * P
    RING = 8
    assert NB % 2 == 0 and 0 < TAIL < P and TB < P

    SPARE = N
    PAD = SPARE + KB * P
    ROWS = -(-(PAD + 2 * P) // P) * P
    ZD = 32
    ZC = ROWS * M // P // ZD
    assert ZC * ZD * P == ROWS * M

    G = 8
    WIN = G * P
    NW = -(-N // WIN)
    WPAIRS = NW // 2
    LASTP = (N - (NW - 1) * WIN) // G
    assert NW % 2 == 0 and N % G == 0

    table = nc.dram_tensor("table", (ROWS, M), F32, kind="Internal").ap()
    numbers = nc.dram_tensor("numbers", (2, NT * P), I32, kind="Internal").ap()
    table_flat = table.rearrange("(p a) m -> p (a m)", p=P)

    with ExitStack() as ctx:
        def sb(name, shape, dt=F32):
            return ctx.enter_context(nc.sbuf_tensor(name, shape, dt))

        def sem(name):
            return ctx.enter_context(nc.semaphore(name))

        def sems(name):
            return [sem(f"{name}{s}") for s in range(2)]

        bank = [ctx.enter_context(nc.psum_tensor(f"bank{b}", [P, 512], F32)) for b in range(8)]

        ident = sb("ident", [P, P])
        earlier = sb("earlier", [P, KB * P])
        spare = sb("spare", [P, KB])
        eps = sb("eps", [P, 1])
        zeros = sb("zeros", [P, ZC])
        w1_ends = sb("w1_ends", [P, 2, M])
        w1_edge = sb("w1_edge", [D, 2, M])
        w2 = sb("w2", [P, 2, M])
        w2t = sb("w2t", [P, 2, M])
        w2n = sb("w2n", [P, 2, M])
        wn1_agg = sb("wn1_agg", [P, M])
        wn1_h = sb("wn1_h", [P, M])
        wn2 = sb("wn2", [P, D])
        b1 = sb("b1", [P, 2])
        b2 = sb("b2", [P, 2])
        b2_wide = sb("b2_wide", [P, 2, P])
        b2n = sb("b2n", [P, KB, M])
        bn1_col = sb("bn1_col", [P, 1])
        bn2_rows = sb("bn2_rows", [P, G, D])

        ends_int = sb("ends_int", [TB, 2, 2, P], I32)
        ends_row = sb("ends_row", [TB, 2, 2, P])
        ends_col = sb("ends_col", [P, NT, 2])

        def two(name, shape, dt=F32):
            return [sb(f"{name}{s}", [P] + shape, dt) for s in range(2)]

        edge_in = two("edge_in", [JT, D])
        others = two("others", [JT, 2, P], I32)
        ids = two("ids", [KB])
        gather_at = [sb(f"gather_at{p}", [P, KB], I32) for p in range(RING)]
        got = [sb(f"got{p}", [P, KB, D]) for p in range(RING)]
        sums = two("sums", [KB])
        centred = two("centred", [KB, D])
        squares = two("squares", [KB, D])
        var = two("var", [KB])
        std = two("std", [KB])
        rstd = two("rstd", [KB])
        h_ends = two("h_ends", [KB, D])
        turned = two("turned", [JT * P])
        turned_edge = [sb(f"turned_edge{s}", [D, JT * P]) for s in range(2)]
        hidden = two("hidden", [2, JT * P])
        message = two("message", [KB, M])
        same = two("same", [KB, KB * P])
        junk = two("junk", [KB, KB * P])
        before = two("before", [KB])
        to_spare = two("to_spare", [KB])
        moved = two("moved", [KB])
        scatter_at = two("scatter_at", [KB], I32)
        to_send = two("to_send", [KB, M])

        nx = two("nx", [G, D])
        ntab = two("ntab", [G, M])
        nsums = two("nsums", [G])
        ncentred = two("ncentred", [G, D])
        nsquares = two("nsquares", [G, D])
        nvar = two("nvar", [G])
        nstd = two("nstd", [G])
        nrstd = two("nrstd", [G])
        nh = two("nh", [G, D])
        nxb = two("nxb", [G, D])
        nxh = two("nxh", [G, D])
        nturned = two("nturned", [G // 2 * P])
        nhidden = two("nhidden", [G * P])
        nout = two("nout", [G, D])

        s_params = sem("params_in")
        s_padded = sem("pad_numbers_written")
        s_ends = sem("ends_in")
        s_numbers = sem("numbers_stored")
        s_zeros = sem("zeros_made")
        s_table0 = sem("table_zeroed")
        s_filled = sem("constants_filled")
        s_const = sem("constants_ready")
        s_rowf = sem("ends_as_float")
        s_b2wide = sem("b2_widened")
        s_setup_pe = sem("setup_products")
        s_setup_ev = sem("setup_copied")

        s_edge_in = sems("edge_in_")
        s_others = sems("others_in_")
        s_gat = [sem(f"gather_at_ready{p}") for p in range(RING)]
        s_got = [sem(f"rows_gathered{p}") for p in range(RING)]
        s_sums = sems("sums_ready")
        s_centred = sems("centred_ready")
        s_squared = sems("squares_ready")
        s_var = sems("var_ready")
        s_std = sems("std_ready")
        s_rstd = sems("rstd_ready")
        s_h = sems("h_ends_ready")
        s_turn = sems("transposed")
        s_turned = sems("turned_ready")
        s_l1 = sems("layer1_done")
        s_hidden = sems("hidden_ready")
        s_l2 = sems("layer2_done")
        s_message = sems("message_ready")
        s_ids = sems("ids_ready")
        s_same = sems("same_ready")
        s_before = sems("before_counted")
        s_tospare = sems("to_spare_ready")
        s_moved = sems("moved_ready")
        s_sat = sems("scatter_at_ready")
        s_joined = sems("joined")
        s_send = sems("to_send_ready")
        s_added = sems("rows_added")

        s_gathers_begun = sem("gathers_begun")
        s_scatters_begun = sem("scatters_begun")

        n_x = sems("n_x_in")
        n_tab = sems("n_table_in")
        n_sums = sems("n_sums_ready")
        n_centred = sems("n_centred_ready")
        n_squared = sems("n_squares_ready")
        n_var = sems("n_var_ready")
        n_std = sems("n_std_ready")
        n_rstd = sems("n_rstd_ready")
        n_h = sems("n_h_ready")
        n_xb = sems("n_x_plus_bias")
        n_xh = sems("n_x_plus_h")
        n_turn = sems("n_transposed")
        n_turned = sems("n_turned_ready")
        n_l1 = sems("n_layer1_done")
        n_hidden = sems("n_hidden_ready")
        n_l2 = sems("n_layer2_done")
        n_out = sems("n_out_ready")
        n_stored = sems("n_stored")

        N_PARAMS = 17

        block = ctx.enter_context(nc.Block())

        def first(i):
            return isinstance(i, int) and i == 0

        @block.sync
        def _(sp):
            def param(to, of):
                sp.dma_start(to, of).then_inc(s_params, 16)

            sp.wait_ge(s_padded, 2)
            for end, a in ((SRC, src), (DST, dst)):
                full = TB * P
                rest = (TB - 1) * P
                sp.dma_start(ends_int[:, end, 0, :], a[0:full].rearrange("(t p) -> t p", p=P)).then_inc(s_ends, 16)
                sp.dma_start(ends_int[0:TB - 1, end, 1, :],
                             a[full:full + rest].rearrange("(t p) -> t p", p=P)).then_inc(s_ends, 16)
                sp.dma_start(ends_int[TB - 1:TB, end, 1, 0:TAIL],
                             a[full + rest:E].rearrange("(t p) -> t p", t=1)).then_inc(s_ends, 16)
            param(w2[:, 0, :], W2_r)
            param(w2[:, 1, :], W2_f)
            param(wn1_agg[:, :], Wn1[0:M, :])
            param(b2[:, 0:1], b2_r.rearrange("(p a) -> p a", a=1))
            param(b2[:, 1:2], b2_f.rearrange("(p a) -> p a", a=1))
            param(w1_ends[:, 1, :], W1_f[0:2 * D, :])
            param(w1_ends[0:D, 0, :], W1_r[D:2 * D, :])
            param(w1_ends[D:2 * D, 0, :], W1_r[0:D, :])
            param(w1_edge[:, 0, :], W1_r[2 * D:3 * D, :])
            param(w1_edge[:, 1, :], W1_f[2 * D:3 * D, :])
            param(b1[:, 0:1], b1_r.rearrange("(p a) -> p a", a=1))
            param(b1[:, 1:2], b1_f.rearrange("(p a) -> p a", a=1))
            param(wn1_h[0:D, :], Wn1[M:M + D, :])
            param(wn1_h[D:2 * D, :], Wn1[M:M + D, :])
            param(wn2[:, :], Wn2)
            sp.wait_ge(s_ends, 6 * 16)
            for end in (SRC, DST):
                sp.dma_start(numbers[end, :].rearrange("(b t p) -> t b p", b=2, p=P),
                             ends_int[:, end, :, :]).then_inc(s_numbers, 16)
            sp.wait_ge(s_numbers, 32)

            def load(i, s):
                last = isinstance(i, int) and i == PAIRS - 1 and s == 1
                first_edge = (2 * i + s) * (JT * P)
                if not first(i):
                    sp.wait_ge(s_turn[s], i)
                    sp.wait_ge(s_same[s], i)
                if last:
                    sp.dma_start(edge_in[s][:, 0, :],
                                 edge_attr[first_edge:first_edge + P, :]).then_inc(s_edge_in[s], 16)
                    sp.dma_start(edge_in[s][0:TAIL, 1, :], edge_attr[first_edge + P:E, :]).then_inc(s_edge_in[s], 16)
                else:
                    sp.dma_start(edge_in[s][:, :, :], edge_attr[bass.ds(first_edge, JT * P), :]
                                 .rearrange("(j p) d -> p j d", p=P)).then_inc(s_edge_in[s], 16)
                for end in (SRC, DST):
                    sp.dma_start(others[s][:, :, end, :],
                                 numbers[end:end + 1, bass.ds(first_edge, JT * P)]
                                 .rearrange("a (j p) -> a j p", p=P).to_broadcast([P, JT, P])
                                 ).then_inc(s_others[s], 16)

            walk(sp, NB, 2, 1, 0, lambda w: w.do(load))

            def node_rows(a, i, s):
                return a[bass.ds((2 * i + s) * WIN, WIN), :].rearrange("(p g) d -> p (g d)", g=G)

            def is_last(i, s):
                return isinstance(i, int) and i == WPAIRS - 1 and s == 1

            def last_rows(a):
                return a[(NW - 1) * WIN:N, :].rearrange("(p g) d -> p (g d)", g=G)

            def load_x(i, s):
                if not first(i):
                    sp.wait_ge(n_centred[s], i)
                    sp.wait_ge(n_xb[s], i)
                to = nx[s][:, :, :].rearrange("p g d -> p (g d)")
                if is_last(i, s):
                    sp.dma_start(to[0:LASTP, :], last_rows(x)).then_inc(n_x[s], 16)
                else:
                    sp.dma_start(to, node_rows(x, i, s)).then_inc(n_x[s], 16)

            def load_table(i, s):
                if not first(i):
                    sp.wait_ge(n_l1[s], 2 * i)
                to = ntab[s][:, :, :].rearrange("p g d -> p (g d)")
                if is_last(i, s):
                    sp.dma_start(to[0:LASTP, :], last_rows(table[0:N, :])).then_inc(n_tab[s], 16)
                else:
                    sp.dma_start(to, node_rows(table, i, s)).then_inc(n_tab[s], 16)

            def store(i, s):
                sp.wait_ge(n_out[s], i + 1)
                of = nout[s][:, :, :].rearrange("p g d -> p (g d)")
                if is_last(i, s):
                    sp.dma_start(last_rows(out), of[0:LASTP, :]).then_inc(n_stored[s], 16)
                else:
                    sp.dma_start(node_rows(out, i, s), of).then_inc(n_stored[s], 16)

            for s in range(2):
                load_x(0, s)
            for s in range(2):
                sp.wait_ge(s_added[s], 16 * KB * PAIRS)
            load_table(0, 0)

            def window(w):
                w.do(load_x, 2)
                w.do(load_table, 1)
                w.do(store, -1)

            walk(sp, NW, 2, 3, 1, window)
            for s in range(2):
                sp.wait_ge(n_stored[s], 16 * WPAIRS)

        @block.gpsimd
        def _(pool):
            for end in (SRC, DST):
                pool.iota(ends_int[:, end, :, :], pattern=[[0, 2], [1, P]], base=PAD + end * P,
                          channel_multiplier=0).then_inc(s_padded, 1)
            pool.iota(spare[:, :], pattern=[[P, KB]], base=SPARE, channel_multiplier=1,
                      allow_small_or_imprecise_dtypes=True).then_inc(s_const, 1)
            pool.memset(ident[:, :], 0.0).then_inc(s_filled, 1)
            pool.memset(earlier[:, :], 1.0).then_inc(s_filled, 1)
            pool.wait_ge(s_filled, 2)
            pool.affine_select(out=ident[:, :], in_=ident[:, :], compare_op=ALU.not_equal, fill=1.0, base=0,
                               pattern=[[-1, P]], channel_multiplier=1).then_inc(s_const, 1)
            tail = earlier[:, (KB - 1) * P:]
            pool.affine_select(out=tail, in_=tail, compare_op=ALU.is_gt, fill=0.0, base=0,
                               pattern=[[-1, P]], channel_multiplier=1).then_inc(s_const, 1)

            def gather(turn, place, read=None):
                pool.wait_ge(s_gat[place], turn + 1)
                if read:
                    i, s = read
                    pool.wait_ge(s_centred[s], i + 1)
                pool.sem_inc(s_gathers_begun, 1)
                for k in range(KB):
                    pool.indirect_dma_start(got[place][:, k, :], None, x,
                                            bass.IndirectOffsetOnAxis(ap=gather_at[place][:, k:k + 1], axis=0)
                                            ).then_inc(s_got[place], 16)

            def scatter(i, s):
                pool.wait_ge(s_sat[s], i + 1)
                pool.wait_ge(s_send[s], i + 1)
                if s == 1:
                    pool.wait_ge(s_added[0], 16 * KB * (i + 1))
                elif not first(i):
                    pool.wait_ge(s_added[1], 16 * KB * i)
                else:
                    pool.wait_ge(s_table0, 16 * ZD)
                pool.sem_inc(s_scatters_begun, 1)
                for k in range(KB):
                    pool.indirect_dma_start(table, bass.IndirectOffsetOnAxis(ap=scatter_at[s][:, k:k + 1], axis=0),
                                            to_send[s][:, k, :], None, compute_op=ALU.add).then_inc(s_added[s], 16)

            for place in range(RING):
                gather(0, place)

            def batch(w):
                w.do(scatter)
                if w.there(RING):
                    gather(*w.ring(RING), read=w.at(0))

            walk(pool, NB, RING, RING, 0, batch)

            def sum_x(i, s):
                pool.wait_ge(n_x[s], 16 * (i + 1))
                if first(i) and s == 0:
                    pool.wait_ge(s_params, 16 * N_PARAMS)
                pool.tensor_tensor(nxb[s][:, :, :], nx[s][:, :, :], bn2_rows[:, :, :], ALU.add).then_inc(n_xb[s], 1)
                pool.wait_ge(n_xb[s], i + 1)
                pool.wait_ge(n_h[s], i + 1)
                if not first(i):
                    pool.wait_ge(n_out[s], i)
                pool.tensor_tensor(nxh[s][:, :, :], nxb[s][:, :, :], nh[s][:, :, :], ALU.add).then_inc(n_xh[s], 1)

            walk(pool, NW, 2, 0, 0, lambda w: w.do(sum_x))

        @block.scalar
        def _(act):
            act.dma_start(bn1_col[:, :], bn1.rearrange("(p a) -> p a", a=1)).then_inc(s_params, 16)
            act.dma_start(bn2_rows[:, :, :], bn2.rearrange("(a b d) -> a b d", a=1, b=1)
                          .to_broadcast([P, G, D])).then_inc(s_params, 16)
            act.wait_ge(s_zeros, 1)
            for z in range(ZD):
                act.dma_start(table_flat[:, z * ZC:(z + 1) * ZC],
                              zeros[:, :]).then_inc(s_table0, 16)

            def square(i, s):
                act.wait_ge(s_centred[s], i + 1)
                if not first(i):
                    act.wait_ge(s_var[s], i)
                act.activation(squares[s][:, :, :], centred[s][:, :, :], ACT.Square,
                               scale=D ** -0.5).then_inc(s_squared[s], 1)

            def root(i, s):
                act.wait_ge(s_var[s], i + 1)
                act.activation(std[s][:, :], var[s][:, :], ACT.Sqrt, bias=eps[:, 0:1]).then_inc(s_std[s], 1)

            def copy_turned(i, s):
                act.wait_ge(s_turn[s], i + 1)
                if not first(i):
                    act.wait_ge(s_l1[s], i)
                act.copy(turned[s][:, :], bank[s][:, 0:JT * P]).then_inc(s_turned[s], 1)
                act.copy(turned_edge[s][:, :], bank[s][0:D, JT * P:2 * JT * P]).then_inc(s_turned[s], 1)

            def relu(i, s):
                act.wait_ge(s_l1[s], i + 1)
                if not first(i):
                    act.wait_ge(s_l2[s], i)
                for end in (SRC, DST):
                    act.activation(hidden[s][:, end, :], bank[2 + s][:, end * JT * P:(end + 1) * JT * P], ACT.Relu,
                                   bias=b1[:, end:end + 1]).then_inc(s_hidden[s], 1)

            def copy_sums(i, s):
                act.wait_ge(s_joined[s], i + 1)
                if not first(i):
                    act.wait_ge(s_added[s], 16 * KB * i)
                act.copy(to_send[s][:, :, :].rearrange("p k m -> p (k m)"), bank[6 + s][:, :]).then_inc(s_send[s], 1)

            def batch(w):
                w.do(root)
                w.do(square, 1)
                w.do(copy_sums, -3)
                w.do(relu, -1)
                w.do(copy_turned)

            act.wait_ge(s_params, 16 * N_PARAMS)
            square(0, 0)
            walk(act, NB, RING, 1, 3, batch)

            def square_nodes(i, s):
                act.wait_ge(n_centred[s], i + 1)
                if not first(i):
                    act.wait_ge(n_var[s], i)
                act.activation(nsquares[s][:, :, :], ncentred[s][:, :, :], ACT.Square,
                               scale=D ** -0.5).then_inc(n_squared[s], 1)

            def root_nodes(i, s):
                act.wait_ge(n_var[s], i + 1)
                act.activation(nstd[s][:, :], nvar[s][:, :], ACT.Sqrt, bias=eps[:, 0:1]).then_inc(n_std[s], 1)

            def copy_nodes(i, s):
                act.wait_ge(n_turn[s], i + 1)
                if not first(i):
                    act.wait_ge(n_l1[s], 2 * i)
                act.copy(nturned[s][:, :], bank[s][:, :]).then_inc(n_turned[s], 1)

            def relu_nodes(i, s):
                for half in range(2):
                    act.wait_ge(n_l1[s], 2 * i + 1 + half)
                    if not first(i):
                        act.wait_ge(n_l2[s], i)
                    act.activation(nhidden[s][:, half * 512:half * 512 + 512], bank[2 + 2 * s + half][:, :], ACT.Relu,
                                   bias=bn1_col[:, 0:1]).then_inc(n_hidden[s], 1)

            def window(w):
                w.do(root_nodes)
                w.do(square_nodes, 1)
                w.do(relu_nodes, -1)
                w.do(copy_nodes)

            square_nodes(0, 0)
            walk(act, NW, 2, 1, 1, window)

        @block.tensor
        def _(pe):
            pe.wait_ge(s_const, 3)
            pe.wait_ge(s_rowf, 1)
            for end in (SRC, DST):
                for b in range(2):
                    c = (2 * end + b) * TB
                    last = pe.transpose(bank[0][:, c:c + TB], ends_row[:, end, b, :], ident[0:TB, 0:TB])
            last.then_inc(s_setup_pe, 1)
            pe.wait_ge(s_params, 16 * N_PARAMS)
            for end in (SRC, DST):
                last = pe.transpose(bank[1][:, end * M:(end + 1) * M], w2[:, end, :], ident[:, :])
            last.then_inc(s_setup_pe, 1)
            pe.wait_ge(s_setup_ev, 3)
            pe.wait_ge(s_b2wide, 2)
            for end in (SRC, DST):
                pe.matmul(bank[2][:, end * M:(end + 1) * M], w2t[:, end, :], wn1_agg[:, :], start=True, stop=True)
            for end in (SRC, DST):
                last = pe.matmul(bank[2][:, (2 + end) * M:(3 + end) * M], b2_wide[:, end, :], wn1_agg[:, :],
                                 start=True, stop=True)
            last.then_inc(s_setup_pe, 1)
            pe.wait_ge(s_setup_ev, 6)

            def turn(i, s):
                if not first(i):
                    pe.wait_ge(s_turned[s], 2 * i)
                if isinstance(i, int) and i == PAIRS - 1 and s == 1:
                    pe.wait_ge(s_edge_in[s], 16 * (i + 2))
                else:
                    pe.wait_ge(s_edge_in[s], 16 * (i + 1))
                pe.wait_ge(s_h[s], i + 1)
                for j in range(JT):
                    pe.transpose(bank[s][:, j * P:(j + 1) * P],
                                 h_ends[s][:, 2 * j:2 * j + 2, :].rearrange("p k d -> p (k d)"), ident[:, :])
                for j in range(JT):
                    last = pe.transpose(bank[s][0:D, (JT + j) * P:(JT + j + 1) * P], edge_in[s][:, j, :], ident[:, :])
                last.then_inc(s_turn[s], 1)

            def layer1(i, s):
                pe.wait_ge(s_turned[s], 2 * (i + 1))
                if not first(i):
                    pe.wait_ge(s_hidden[s], 2 * i)
                for end in (SRC, DST):
                    c = end * JT * P
                    pe.matmul(bank[2 + s][:, c:c + JT * P], w1_ends[:, end, :], turned[s][:, 0:JT * P],
                              start=True, stop=False)
                    last = pe.matmul(bank[2 + s][:, c:c + JT * P], w1_edge[:, end, :], turned_edge[s][:, :],
                                     start=False, stop=True)
                last.then_inc(s_l1[s], 1)

            def layer2(i, s):
                if not first(i):
                    pe.wait_ge(s_message[s], i)
                for end in (SRC, DST):
                    pe.wait_ge(s_hidden[s], 2 * i + 1 + end)
                    for j in range(JT):
                        k = 2 * j + end
                        last = pe.matmul(bank[4 + s][:, k * M:(k + 1) * M], hidden[s][:, end, j * P:(j + 1) * P],
                                         w2n[:, end, :], start=True, stop=True)
                last.then_inc(s_l2[s], 1)

            def join(i, s):
                pe.wait_ge(s_message[s], i + 1)
                pe.wait_ge(s_same[s], i + 1)
                if not first(i):
                    pe.wait_ge(s_send[s], i)
                for k in range(KB):
                    for o in range(KB):
                        last = pe.matmul(bank[6 + s][:, k * M:(k + 1) * M], same[s][:, o, k * P:(k + 1) * P],
                                         message[s][:, o, :], start=(o == 0), stop=(o == KB - 1))
                last.then_inc(s_joined[s], 1)

            def batch(w):
                w.do(turn)
                w.do(layer2, -1)
                w.do(layer1)
                w.do(join, -2)

            walk(pe, NB, 4, 1, 2, batch)

            for s in range(2):
                pe.wait_ge(s_send[s], PAIRS)
                pe.wait_ge(s_message[s], PAIRS)

            def turn_nodes(i, s):
                pe.wait_ge(n_h[s], i + 1)
                if not first(i):
                    pe.wait_ge(n_turned[s], i)
                for q in range(G // 2):
                    last = pe.transpose(bank[s][:, q * P:(q + 1) * P],
                                        nh[s][:, 2 * q:2 * q + 2, :].rearrange("p g d -> p (g d)"), ident[:, :])
                last.then_inc(n_turn[s], 1)

            def layer1_nodes(i, s):
                pe.wait_ge(n_tab[s], 16 * (i + 1))
                pe.wait_ge(n_turned[s], i + 1)
                if not first(i):
                    pe.wait_ge(n_hidden[s], 2 * i)
                for odd in range(2):
                    for q in range(G // 2):
                        pe.matmul(bank[2 + 2 * s + odd][:, q * P:(q + 1) * P], ntab[s][:, 2 * q + odd, :], ident[:, :],
                                  start=(q == 0), stop=False, is_transpose=True)
                for odd in range(2):
                    pe.matmul(bank[2 + 2 * s + odd][:, :], wn1_h[odd * D:(odd + 1) * D, :],
                              nturned[s][odd * D:(odd + 1) * D, :], start=False, stop=True).then_inc(n_l1[s], 1)

            def layer2_nodes(i, s):
                if not first(i):
                    pe.wait_ge(n_out[s], i)
                for odd in range(2):
                    pe.wait_ge(n_hidden[s], 2 * i + 1 + odd)
                    for q in range(G // 2):
                        g, c = 2 * q + odd, (odd * (G // 2) + q) * P
                        last = pe.matmul(bank[6 + s][:, g * D:(g + 1) * D], nhidden[s][:, c:c + P], wn2[:, :],
                                         start=True, stop=True)
                last.then_inc(n_l2[s], 1)

            def window(w):
                w.do(turn_nodes)
                w.do(layer2_nodes, -1)
                w.do(layer1_nodes)

            walk(pe, NW, 2, 0, 1, window)

        @block.vector
        def _(dve):
            dve.memset(zeros[:, :], 0.0).then_inc(s_zeros, 1)
            dve.memset(eps[:, :], EPS).then_inc(s_const, 1)
            dve.wait_ge(s_ends, 6 * 16)
            dve.tensor_copy(ends_row[:, :, :, :], ends_int[:, :, :, :]).then_inc(s_rowf, 1)
            dve.wait_ge(s_setup_pe, 1)
            for end in (SRC, DST):
                dve.tensor_copy(ends_col[:, :, end], bank[0][:, 2 * end * TB:(2 * end + 2) * TB]
                                ).then_inc(s_setup_ev, 1)
            dve.wait_ge(s_params, 16 * N_PARAMS)
            for end in (SRC, DST):
                dve.tensor_copy(b2_wide[:, end, :], b2[:, end:end + 1].to_broadcast([P, P])).then_inc(s_b2wide, 1)
            dve.wait_ge(s_setup_pe, 2)
            dve.tensor_copy(w2t[:, :, :].rearrange("p a m -> p (a m)"), bank[1][:, 0:2 * M]).then_inc(s_setup_ev, 1)
            dve.wait_ge(s_setup_pe, 3)
            dve.tensor_copy(w2n[:, :, :].rearrange("p a m -> p (a m)"), bank[2][:, 0:2 * M]).then_inc(s_setup_ev, 1)
            for j in range(JT):
                dve.tensor_copy(b2n[:, 2 * j:2 * j + 2, :].rearrange("p a m -> p (a m)"),
                                bank[2][:, 2 * M:4 * M]).then_inc(s_setup_ev, 1)
            dve.wait_ge(s_setup_ev, 6)
            dve.wait_ge(s_const, 4)

            ends = ends_col[:, :, :].rearrange("p t e -> p (t e)")

            def gather_rows(turn, place):
                dve.tensor_scalar(gather_at[place][:, :], ends[:, bass.ds((RING * turn + place) * KB, KB)],
                                  float(N - 1), None, ALU.min).then_inc(s_gat[place], 1)

            def centre(i, s, turn, place):
                dve.wait_ge(s_got[place], 16 * KB * (turn + 1))
                dve.tensor_reduce(sums[s][:, :], got[place][:, :, :], AX.X, ALU.add).then_inc(s_sums[s], 1)
                dve.wait_ge(s_sums[s], i + 1)
                dve.scalar_tensor_tensor(out=centred[s][:, :, :], in0=sums[s][:, :].to_broadcast([P, KB, D]),
                                         scalar=-1.0 / D, in1=got[place][:, :, :], op0=ALU.mult, op1=ALU.add
                                         ).then_inc(s_centred[s], 1)

            def match(i, s):
                if not first(i):
                    dve.wait_ge(s_sat[s], i)
                dve.tensor_copy(ids[s][:, :], ends[:, bass.ds((2 * i + s) * KB, KB)]).then_inc(s_ids[s], 1)
                dve.wait_ge(s_ids[s], i + 1)
                dve.wait_ge(s_others[s], 32 * (i + 1))
                if not first(i):
                    dve.wait_ge(s_joined[s], i)
                row = others[s][:, :, :, :].rearrange("p j e q -> p (j e q)")
                for o in range(KB):
                    last = dve.tensor_scalar(same[s][:, o, :], row, ids[s][:, o:o + 1], None, ALU.is_equal)
                last.then_inc(s_same[s], 1)

            def variance(i, s):
                dve.wait_ge(s_squared[s], i + 1)
                dve.tensor_reduce(var[s][:, :], squares[s][:, :, :], AX.X, ALU.add).then_inc(s_var[s], 1)

            def targets(i, s):
                dve.wait_ge(s_same[s], i + 1)
                for k in range(KB):
                    w = (k + 1) * P
                    last = dve.tensor_tensor_reduce(junk[s][:, k, 0:w], same[s][:, k, 0:w], earlier[:, KB * P - w:],
                                                    1.0, 0.0, ALU.mult, ALU.add, before[s][:, k:k + 1])
                last.then_inc(s_before[s], 1)
                dve.tensor_tensor(to_spare[s][:, :], spare[:, :], ids[s][:, :], ALU.subtract).then_inc(s_tospare[s], 1)
                dve.wait_ge(s_before[s], i + 1)
                dve.wait_ge(s_tospare[s], i + 1)
                dve.scalar_tensor_tensor(out=moved[s][:, :], in0=before[s][:, :], scalar=1.0, in1=to_spare[s][:, :],
                                         op0=ALU.min, op1=ALU.mult).then_inc(s_moved[s], 1)
                dve.wait_ge(s_moved[s], i + 1)
                if not first(i):
                    dve.wait_ge(s_added[s], 16 * KB * i)
                dve.tensor_tensor(scatter_at[s][:, :], moved[s][:, :], ids[s][:, :], ALU.add).then_inc(s_sat[s], 1)

            def messages(i, s):
                dve.wait_ge(s_l2[s], i + 1)
                if not first(i):
                    dve.wait_ge(s_joined[s], i)
                dve.tensor_tensor(message[s][:, :, :].rearrange("p k m -> p (k m)"), bank[4 + s][:, :],
                                  b2n[:, :, :].rearrange("p k m -> p (k m)"), ALU.add).then_inc(s_message[s], 1)

            def normal(i, s):
                dve.wait_ge(s_std[s], i + 1)
                dve.reciprocal(rstd[s][:, :], std[s][:, :]).then_inc(s_rstd[s], 1)
                dve.wait_ge(s_rstd[s], i + 1)
                if not first(i):
                    dve.wait_ge(s_turn[s], i)
                dve.scalar_tensor_tensor(out=h_ends[s][:, :, :], in0=centred[s][:, :, :], scalar=0.0,
                                         in1=rstd[s][:, :].to_broadcast([P, KB, D]), op0=ALU.max, op1=ALU.mult
                                         ).then_inc(s_h[s], 1)

            def batch(w):
                w.do(variance)
                if w.there(1):
                    centre(*w.at(1), *w.ring(1))
                if w.there(RING):
                    gather_rows(*w.ring(RING))
                w.do(normal)
                w.do(messages, -1)
                w.do(match, -1)
                w.do(targets, -1)

            for place in range(RING):
                gather_rows(0, place)
            centre(0, 0, 0, 0)
            walk(dve, NB, RING, RING, 1, batch)

            def centre_nodes(i, s):
                dve.wait_ge(n_x[s], 16 * (i + 1))
                dve.tensor_reduce(nsums[s][:, :], nx[s][:, :, :], AX.X, ALU.add).then_inc(n_sums[s], 1)
                dve.wait_ge(n_sums[s], i + 1)
                dve.scalar_tensor_tensor(out=ncentred[s][:, :, :], in0=nsums[s][:, :].to_broadcast([P, G, D]),
                                         scalar=-1.0 / D, in1=nx[s][:, :, :], op0=ALU.mult, op1=ALU.add
                                         ).then_inc(n_centred[s], 1)

            def output(i, s):
                dve.wait_ge(n_l2[s], i + 1)
                dve.wait_ge(n_xh[s], i + 1)
                if not first(i):
                    dve.wait_ge(n_stored[s], 16 * i)
                dve.tensor_tensor(nout[s][:, :, :].rearrange("p g d -> p (g d)"), bank[6 + s][:, :],
                                  nxh[s][:, :, :].rearrange("p g d -> p (g d)"), ALU.add).then_inc(n_out[s], 1)

            def variance_nodes(i, s):
                dve.wait_ge(n_squared[s], i + 1)
                dve.tensor_reduce(nvar[s][:, :], nsquares[s][:, :, :], AX.X, ALU.add).then_inc(n_var[s], 1)

            def normal_nodes(i, s):
                dve.wait_ge(n_std[s], i + 1)
                dve.reciprocal(nrstd[s][:, :], nstd[s][:, :]).then_inc(n_rstd[s], 1)
                dve.wait_ge(n_rstd[s], i + 1)
                if not first(i):
                    dve.wait_ge(n_turn[s], i)
                    dve.wait_ge(n_xh[s], i)
                dve.scalar_tensor_tensor(out=nh[s][:, :, :], in0=ncentred[s][:, :, :], scalar=0.0,
                                         in1=nrstd[s][:, :].to_broadcast([P, G, D]), op0=ALU.max, op1=ALU.mult
                                         ).then_inc(n_h[s], 1)

            def window(w):
                w.do(variance_nodes)
                w.do(centre_nodes, 1)
                w.do(normal_nodes)
                w.do(output, -2)

            centre_nodes(0, 0)
            walk(dve, NW, 2, 1, 2, window)


_INS = ['x', 'src', 'dst', 'edge_attr_64', 'L0_gnn_W1_f', 'L0_gnn_b1_f', 'L0_gnn_W2_f', 'L0_gnn_b2_f',
        'L0_gnn_W1_r', 'L0_gnn_b1_r', 'L0_gnn_W2_r', 'L0_gnn_b2_r', 'L0_gnn_Wn1', 'L0_gnn_bn1', 'L0_gnn_Wn2',
        'L0_gnn_bn2']


def kernel(**inputs):
    import numpy as _np
    import concourse.bacc as _bacc
    from concourse import mybir as _mybir
    from concourse.bass_utils import run_bass_kernel_spmd as _run

    nc = _bacc.Bacc("TRN2", target_bir_lowering=False, num_devices=1)
    arrays, args = {}, []
    for name in _INS:
        a = _np.ascontiguousarray(inputs[name])
        arrays[f"in_{name}"] = a
        args.append(nc.dram_tensor(f"in_{name}", a.shape, _mybir.dt.from_np(a.dtype), kind="ExternalInput").ap())
    out = nc.dram_tensor("out_x", inputs["x"].shape, _mybir.dt.float32, kind="ExternalOutput").ap()
    gnn_layer(nc, *args, out)
    r = _run(nc, [arrays], core_ids=[0])
    return r.results[0]["out_x"]
```

```python
from contextlib import ExitStack

import concourse.bass as bass
from concourse import mybir

F32 = mybir.dt.float32
I32 = mybir.dt.int32
ALU = mybir.AluOpType
ACT = mybir.ActivationFunctionType
AX = mybir.AxisListType

P = 128
EPS = 1e-5


class Step:

    def __init__(self, count, n, base=0, unroll=1, turn=None):
        self.count, self.n, self.base, self.unroll, self.turn = count, n, base, unroll, turn

    def number(self, k=0):
        return self.n + k if self.turn is None else self.turn * self.unroll + (self.base + self.n + k)

    def least(self, k=0):
        return self.base + self.n + k

    def there(self, k=0):
        return self.turn is not None or 0 <= self.n + k < self.count

    def of(self, size, k=0):
        use, place = divmod(self.n + k, size)
        if self.turn is None:
            return use, place
        return self.turn * (self.unroll // size) + (self.base // size + use), place

    def do(self, stage, k=0, ring=2):
        if self.there(k):
            stage(*self.of(2, k), *(self.of(ring, k) if ring != 2 else ()))


def run(eng, count, loops, behind, body):
    done = 0
    for begin, end, unroll in loops:
        assert begin % unroll == 0 and end % unroll == 0
        for n in range(done, begin):
            body(Step(count, n))
        with eng.Fori(0, (end - begin) // unroll) as turn:
            turn = eng.snap(turn)
            for n in range(unroll):
                body(Step(count, n, begin, unroll, turn))
        done = end
    for n in range(done, count + behind):
        body(Step(count, n))


def gnn_layer(nc, x, src, dst, edge_attr, W1_f, b1_f, W2_f, b2_f, W1_r, b1_r, W2_r, b2_r, Wn1, bn1, Wn2, bn2, out):
    N, D = x.shape
    E = src.shape[0]
    M = W2_f.shape[1]
    assert D == 64 and M == P
    SRC, DST = 0, 1

    JT = 2
    KB = 2 * JT
    NT = -(-E // (P * JT)) * JT
    NB = NT // JT
    PAIRS = NB // 2
    TB = NT // 2
    TAIL = E - (NT - 1) * P
    RING = 4
    assert NB % 2 == 0 and 0 < TAIL < P and TB < P

    SPARE = N
    PAD = SPARE + KB * P
    ROWS = -(-(PAD + 2 * P) // P) * P
    ZC = (ROWS - N) * M // P

    G = 8
    WIN = G * P
    NW = -(-N // WIN)
    NRING = 4
    LASTP = (N - (NW - 1) * WIN) // G
    KEPT = NW // NRING
    MORE = 10
    MORE_FROM = KEPT - MORE
    assert NW % 2 == 0 and N % G == 0 and G * D == 2 * KB * D and 2 * KEPT <= PAIRS and 4 * KEPT <= NB

    table = nc.dram_tensor("table", (ROWS, M), F32, kind="Internal").ap()
    numbers = nc.dram_tensor("numbers", (2, NT * P), I32, kind="Internal").ap()
    behind_nodes = table[N:ROWS, :].rearrange("r m -> (r m)").rearrange("(p c) -> p c", p=P)

    with ExitStack() as ctx:
        def sb(name, shape, dt=F32):
            return ctx.enter_context(nc.sbuf_tensor(name, shape, dt))

        def sem(name):
            return ctx.enter_context(nc.semaphore(name))

        def sems(name):
            return [sem(f"{name}{s}") for s in range(2)]

        bank = [ctx.enter_context(nc.psum_tensor(f"bank{b}", [P, 512], F32)) for b in range(8)]

        ident = sb("ident", [P, P])
        earlier = sb("earlier", [P, KB * P])
        spare = sb("spare", [P, KB])
        eps = sb("eps", [P, 1])
        zeros = sb("zeros", [P, ZC])
        w1_ends = sb("w1_ends", [P, 2, M])
        w1_edge = sb("w1_edge", [D, 2, M])
        w2 = sb("w2", [P, 2, M])
        w2t = sb("w2t", [P, 2, M])
        w2n = sb("w2n", [P, 2, M])
        wn1_agg = sb("wn1_agg", [P, M])
        wn1_h = sb("wn1_h", [P, 2, M])
        wn2 = sb("wn2", [P, D])
        b1 = sb("b1", [P, 2])
        b2 = sb("b2", [P, 2])
        b2_wide = sb("b2_wide", [P, 2, P])
        b2n = sb("b2n", [P, KB, M])
        bn1_col = sb("bn1_col", [P, 1])
        bn2_rows = sb("bn2_rows", [P, G, D])

        ends_int = sb("ends_int", [TB, 2, 2, P], I32)
        ends_row = sb("ends_row", [TB, 2, 2, P])
        ends_col = sb("ends_col", [P, NT, 2])

        def two(name, shape, dt=F32):
            return [sb(f"{name}{s}", [P] + shape, dt) for s in range(2)]

        edge_in = two("edge_in", [JT, D])
        others = two("others", [JT, 2, P], I32)
        ids = two("ids", [KB])
        gather_first = sb("gather_first", [P, NB * KB], I32)
        gather_at = [sb(f"gather_at{p}", [P, KB], I32) for p in range(RING)]
        got_even = sb("got_even", [P, PAIRS, KB * D])
        got_odd = [sb(f"got_odd{p}", [P, 1, KB * D]) for p in range(RING)]
        sums = two("sums", [KB])
        centred = two("centred", [KB, D])
        squares = two("squares", [KB, D])
        var = two("var", [KB])
        std = two("std", [KB])
        rstd = two("rstd", [KB])
        h_ends = two("h_ends", [KB, D])
        turned = two("turned", [JT * P])
        turned_edge = [sb(f"turned_edge{s}", [D, JT * P]) for s in range(2)]
        hidden = two("hidden", [2, JT * P])
        message = two("message", [KB, M])
        same = two("same", [KB, KB * P])
        junk = two("junk", [KB, KB * P], mybir.dt.bfloat16)
        before = two("before", [KB])
        to_spare = two("to_spare", [KB])
        moved = two("moved", [KB])
        scatter_at = two("scatter_at", [KB], I32)
        to_send = two("to_send", [KB, M])

        nx = [sb(f"nx{p}", [P, G, D]) for p in range(NRING)]
        ntab = [same[p // 2][:, :, :].rearrange("p a b -> p (a b)")[:, p % 2 * G * M:(p % 2 + 1) * G * M]
                for p in range(NRING)]
        all_sums = sb("all_sums", [P, NW, G])
        all_rstd = sb("all_rstd", [P, NW, G])
        ncentred = two("ncentred", [G, D])
        nsquares = two("nsquares", [G, D])
        nvar = two("nvar", [G])
        nstd = two("nstd", [G])
        nh = [sb(f"nh{p}", [P, G, D]) for p in range(NRING)]
        nxb = two("nxb", [G, D])
        nxh = [sb(f"nxh{p}", [P, G, D]) for p in range(NRING)]
        kept_more = sb("kept_more", [P, MORE, G * D])
        nturned = two("nturned", [G // 2 * P])
        nhidden = two("nhidden", [G * P])
        nout = two("nout", [G, D])

        s_params = sem("params_in")
        s_wn1h = sem("wn1_h_in")
        s_padded = sem("pad_numbers_written")
        s_ends = sem("ends_in")
        s_numbers = sem("numbers_stored")
        s_zeros = sem("zeros_made")
        s_table0 = sem("behind_nodes_zeroed")
        s_filled = sem("constants_filled")
        s_const = sem("constants_ready")
        s_rowf = sem("ends_as_float")
        s_b2wide = sem("b2_widened")
        s_setup_pe = sem("setup_products")
        s_setup_ev = sem("setup_copied")

        s_edge_in = sems("edge_in_")
        s_others = sems("others_in_")
        s_gat = [sem(f"gather_at_ready{p}") for p in range(RING)]
        s_got = [sem(f"rows_gathered{p}") for p in range(RING)]
        s_got_even = sem("even_rows_gathered")
        s_first = sem("gather_first_ready")
        s_sums = sems("sums_ready")
        s_centred = sems("centred_ready")
        s_squared = sems("squares_ready")
        s_var = sems("var_ready")
        s_std = sems("std_ready")
        s_rstd = sems("rstd_ready")
        s_h = sems("h_ends_ready")
        s_turn = sems("transposed")
        s_turned = sems("turned_ready")
        s_l1 = sems("layer1_done")
        s_hidden = sems("hidden_ready")
        s_l2 = sems("layer2_done")
        s_message = sems("message_ready")
        s_ids = sems("ids_ready")
        s_same = sems("same_ready")
        s_before = sems("before_counted")
        s_tospare = sems("to_spare_ready")
        s_moved = sems("moved_ready")
        s_sat = sems("scatter_at_ready")
        s_joined = sems("joined")
        s_send = sems("to_send_ready")
        s_added = sems("rows_added")

        s_gathers_begun = sem("gathers_begun")
        s_scatters_begun = sem("scatters_begun")

        b_x = [sem(f"b_x_in{p}") for p in range(NRING)]
        b_sums = sems("b_sums_ready")
        b_centred = sems("b_centred_ready")
        b_squared = sems("b_squares_ready")
        b_var = sems("b_var_ready")
        b_std = sems("b_std_ready")
        b_rstd = sems("b_rstd_ready")
        b_h = sems("b_h_ready")
        b_turn = sems("b_transposed")
        b_turned = sems("b_turned_ready")
        b_product = sems("b_product_done")
        b_rows = sems("b_rows_ready")
        b_stored = sems("b_rows_stored")

        s_kept = sem("kept_windows_in")
        n_x = [sem(f"n_x_in{p}") for p in range(NRING - 1)]
        n_tab = [sem(f"n_table_in{p}") for p in range(NRING)]
        n_centred = sems("n_centred_ready")
        n_h = sems("n_h_ready")
        n_xb = sems("n_x_plus_bias")
        n_xh = sems("n_x_plus_h")
        n_turned = sems("n_table_transposed")
        n_hidden = sems("n_hidden_ready")
        n_l2 = sems("n_layer2_done")
        n_out = sems("n_out_ready")
        n_stored = sems("n_stored")

        N_PARAMS = 15

        block = ctx.enter_context(nc.Block())

        def first(i):
            return isinstance(i, int) and i == 0

        def in_ring(w, k):
            place = w.of(NRING, k)[1]
            return not (place == NRING - 1 or place == 1 and MORE_FROM <= w.least(k) // NRING < KEPT)

        def wait_for_x(eng, w, k):
            turn, place = w.of(NRING, k)
            if in_ring(w, k):
                missing = MORE if place == 1 and w.least(k) // NRING >= KEPT else 0
                eng.wait_ge(n_x[place], 16 * (turn + 1 - missing))
            elif first(turn):
                eng.wait_ge(s_kept, 16 * (KEPT + MORE))

        def window_of_x(w, k):
            turn, place = w.of(NRING, k)
            if in_ring(w, k):
                return nx[place][:, :, :]
            if place == 1:
                return kept_more[:, bass.ds(turn - MORE_FROM, 1), :].rearrange("p a (g d) -> p (a g) d", d=D)
            return got_even[:, bass.ds(2 * turn, 2), :].rearrange("p a (g d) -> p (a g) d", d=D)

        @block.sync
        def _(sp):
            def param(to, of):
                sp.dma_start(to, of).then_inc(s_params, 16)

            def set_up():
                for k in range(NRING):
                    Step(NW, 0).do(load_x_begin, k, ring=NRING)
                for half in range(2):
                    sp.dma_start(wn1_h[half * D:(half + 1) * D, half, :], Wn1[M:M + D, :]).then_inc(s_wn1h, 16)
                sp.wait_ge(s_padded, 2)
                full = TB * P
                rest = (TB - 1) * P
                for end, a in ((SRC, src), (DST, dst)):
                    sp.dma_start(ends_int[:, end, 0, :], a[0:full].rearrange("(t p) -> t p", p=P)).then_inc(s_ends, 16)
                    sp.dma_start(ends_int[0:TB - 1, end, 1, :],
                                 a[full:full + rest].rearrange("(t p) -> t p", p=P)).then_inc(s_ends, 16)
                    sp.dma_start(ends_int[TB - 1:TB, end, 1, 0:TAIL],
                                 a[full + rest:E].rearrange("(t p) -> t p", t=1)).then_inc(s_ends, 16)
                param(w2[:, 0, :], W2_r)
                param(w2[:, 1, :], W2_f)
                param(wn1_agg[:, :], Wn1[0:M, :])
                param(b2[:, 0:1], b2_r.rearrange("(p a) -> p a", a=1))
                param(b2[:, 1:2], b2_f.rearrange("(p a) -> p a", a=1))
                param(w1_ends[:, 1, :], W1_f[0:2 * D, :])
                param(w1_ends[0:D, 0, :], W1_r[D:2 * D, :])
                param(w1_ends[D:2 * D, 0, :], W1_r[0:D, :])
                param(w1_edge[:, 0, :], W1_r[2 * D:3 * D, :])
                param(w1_edge[:, 1, :], W1_f[2 * D:3 * D, :])
                param(b1[:, 0:1], b1_r.rearrange("(p a) -> p a", a=1))
                param(b1[:, 1:2], b1_f.rearrange("(p a) -> p a", a=1))
                param(wn2[:, :], Wn2)
                param(bn1_col[:, :], bn1.rearrange("(p a) -> p a", a=1))
                for k in range(NRING, 6):
                    Step(NW, 0).do(load_x_begin, k, ring=NRING)
                param(bn2_rows[:, :, :], bn2.rearrange("(a b d) -> a b d", a=1, b=1).to_broadcast([P, G, D]))
                sp.wait_ge(s_ends, 6 * 16)
                for end in (SRC, DST):
                    sp.dma_start(numbers[end, :].rearrange("(b t p) -> t b p", b=2, p=P),
                                 ends_int[:, end, :, :]).then_inc(s_numbers, 16)

            def load(i, s):
                last = isinstance(i, int) and i == PAIRS - 1 and s == 1
                first_edge = (2 * i + s) * (JT * P)
                if not first(i):
                    sp.wait_ge(s_turn[s], i)
                    sp.wait_ge(s_same[s], i)
                if last:
                    sp.dma_start(edge_in[s][:, 0, :],
                                 edge_attr[first_edge:first_edge + P, :]).then_inc(s_edge_in[s], 16)
                    sp.dma_start(edge_in[s][0:TAIL, 1, :], edge_attr[first_edge + P:E, :]).then_inc(s_edge_in[s], 16)
                else:
                    sp.dma_start(edge_in[s][:, :, :], edge_attr[bass.ds(first_edge, JT * P), :]
                                 .rearrange("(j p) d -> p j d", p=P)).then_inc(s_edge_in[s], 16)
                for end in (SRC, DST):
                    sp.dma_start(others[s][:, :, end, :],
                                 numbers[end:end + 1, bass.ds(first_edge, JT * P)]
                                 .rearrange("a (j p) -> a j p", p=P).to_broadcast([P, JT, P])
                                 ).then_inc(s_others[s], 16)

            def node_rows(a, i, s):
                return a[bass.ds((2 * i + s) * WIN, WIN), :].rearrange("(p g) d -> p (g d)", g=G)

            def is_last(i, s):
                return isinstance(i, int) and 2 * i + s == NW - 1

            def last_rows(a):
                return a[(NW - 1) * WIN:N, :].rearrange("(p g) d -> p (g d)", g=G)

            def load_window(a, i, s, to, landed):
                if is_last(i, s):
                    sp.dma_start(to[0:LASTP, :], last_rows(a)).then_inc(landed, 16)
                else:
                    sp.dma_start(to, node_rows(a, i, s)).then_inc(landed, 16)

            def store_window(a, i, s, of, stored):
                if is_last(i, s):
                    sp.dma_start(last_rows(a), of[0:LASTP, :]).then_inc(stored, 16)
                else:
                    sp.dma_start(node_rows(a, i, s), of).then_inc(stored, 16)

            def flat(a):
                return a[:, :, :].rearrange("p g d -> p (g d)")

            def load_x_begin(i, s, turn, place):
                if not first(turn):
                    sp.wait_ge(b_centred[s], i - 1)
                load_window(x, i, s, flat(nx[place]), b_x[place])

            def store_rows(i, s):
                sp.wait_ge(b_rows[s], 2 * (i + 1))
                store_window(table[0:N, :], i, s, nhidden[s][:, :], b_stored[s])

            def begin(w):
                w.do(load_x_begin, 6, ring=NRING)
                w.do(store_rows, -1)
                if w.least() == 3:
                    sp.wait_ge(s_numbers, 32)
                    load(0, 0)
                    load(0, 1)
                    sp.wait_ge(s_zeros, 1)
                    sp.dma_start(behind_nodes, zeros[:, :]).then_inc(s_table0, 16)

            set_up()
            run(sp, NW, [(4, 88, 4)], 1, begin)

            def keep_window(v):
                sp.wait_ge(s_centred[0], 2 * v + 2)
                sp.dma_start(got_even[:, bass.ds(2 * v, 2), :].rearrange("p a c -> p (a c)"),
                             x[bass.ds((v * NRING + NRING - 1) * WIN, WIN), :].rearrange("(p g) d -> p (g d)", g=G)
                             ).then_inc(s_kept, 16)

            def batch(w):
                if w.least() >= 2:
                    w.do(load)
                v, rest = w.of(4)
                if rest == 3:
                    keep_window(v)

            for v in range(MORE):
                first_node = ((MORE_FROM + v) * NRING + 1) * WIN
                sp.dma_start(kept_more[:, v, :], x[first_node:first_node + WIN, :]
                             .rearrange("(p g) d -> p (g d)", g=G)).then_inc(s_kept, 16)
            run(sp, NB, [(4, 96, 4)], 0, batch)

            def load_x(w, k):
                if not w.there(k) or not in_ring(w, k):
                    return
                i, s = w.of(2, k)
                turn, place = w.of(NRING, k)
                if not first(turn):
                    sp.wait_ge(n_centred[s], i - 1)
                    sp.wait_ge(n_xb[s], i - 1)
                else:
                    for q in range(2):
                        sp.wait_ge(b_centred[q], NW // 2)
                load_window(x, i, s, flat(nx[place]), n_x[place])

            def load_table(i, s, turn, place):
                if not first(turn):
                    sp.wait_ge(n_turned[s], 2 * (i - 1))
                load_window(table[0:N, :], i, s, ntab[place], n_tab[place])

            def store(i, s):
                sp.wait_ge(n_out[s], i + 1)
                store_window(out, i, s, flat(nout[s]), n_stored[s])

            for k in range(NRING):
                load_x(Step(NW, 0), k)
            for s in range(2):
                sp.wait_ge(s_added[s], 16 * KB * PAIRS)
            for k in range(3):
                Step(NW, 0).do(load_table, k, ring=NRING)
            for k in range(NRING, 6):
                load_x(Step(NW, 0), k)

            def window(w):
                load_x(w, 6)
                w.do(load_table, 3, ring=NRING)
                w.do(store, -1)

            split = (MORE_FROM - 2) * NRING
            run(sp, NW, [(4, split, NRING), (split, 88, NRING)], 1, window)
            for s in range(2):
                sp.wait_ge(n_stored[s], 16 * (NW // 2))

        @block.gpsimd
        def _(pool):
            for end in (SRC, DST):
                pool.iota(ends_int[:, end, :, :], pattern=[[0, 2], [1, P]], base=PAD + end * P,
                          channel_multiplier=0).then_inc(s_padded, 1)
            pool.iota(spare[:, :], pattern=[[P, KB]], base=SPARE, channel_multiplier=1,
                      allow_small_or_imprecise_dtypes=True).then_inc(s_const, 1)
            pool.memset(ident[:, :], 0.0).then_inc(s_filled, 1)
            pool.memset(earlier[:, :], 1.0).then_inc(s_filled, 1)
            pool.wait_ge(s_filled, 2)
            pool.affine_select(out=ident[:, :], in_=ident[:, :], compare_op=ALU.not_equal, fill=1.0, base=0,
                               pattern=[[-1, P]], channel_multiplier=1).then_inc(s_const, 1)
            tail = earlier[:, (KB - 1) * P:]
            pool.affine_select(out=tail, in_=tail, compare_op=ALU.is_gt, fill=0.0, base=0,
                               pattern=[[-1, P]], channel_multiplier=1).then_inc(s_const, 1)

            def gather(to, numbers, landed, tiles=range(KB)):
                for k in tiles:
                    pool.indirect_dma_start(to[:, k * D:(k + 1) * D], None, x,
                                            bass.IndirectOffsetOnAxis(ap=numbers[:, k:k + 1], axis=0)
                                            ).then_inc(landed, 16)

            def scatter(i, s):
                pool.wait_ge(s_sat[s], i + 1)
                pool.wait_ge(s_send[s], i + 1)
                if s == 1:
                    pool.wait_ge(s_added[0], 16 * KB * (i + 1))
                elif not first(i):
                    pool.wait_ge(s_added[1], 16 * KB * i)
                else:
                    pool.wait_ge(s_table0, 16)
                    for q in range(2):
                        pool.wait_ge(b_stored[q], 16 * (NW // 2))
                pool.sem_inc(s_scatters_begun, 1)
                for k in range(KB):
                    pool.indirect_dma_start(table, bass.IndirectOffsetOnAxis(ap=scatter_at[s][:, k:k + 1], axis=0),
                                            to_send[s][:, k, :], None, compute_op=ALU.add).then_inc(s_added[s], 16)

            def gather_odd(w):
                pair = w.of(2, 2 * RING)[0]
                turn, place = w.of(2 * RING, 2 * RING)
                place //= 2
                half = w.n % 2
                if half == 0:
                    pool.wait_ge(s_gat[place], turn)
                    pool.wait_ge(s_centred[1], pair - RING + 1)
                    pool.sem_inc(s_gathers_begun, 1)
                gather(got_odd[place][:, 0, :], gather_at[place], s_got[place],
                       range(half * JT, (half + 1) * JT))

            pool.wait_ge(s_first, 1)
            for i in range(PAIRS):
                if i < RING:
                    gather(got_odd[i][:, 0, :], gather_first[:, (2 * i + 1) * KB:(2 * i + 2) * KB], s_got[i])
                gather(got_even[:, i, :], gather_first[:, 2 * i * KB:(2 * i + 1) * KB], s_got_even)

            def batch(w):
                w.do(scatter)
                if w.there(2 * RING):
                    gather_odd(w)

            run(pool, NB, [(8, 88, 2 * RING)], 0, batch)

            def sum_x(w):
                i, s = w.of(2)
                turn, place = w.of(NRING)
                wait_for_x(pool, w, 0)
                if first(i) and s == 0:
                    pool.wait_ge(s_params, 16 * N_PARAMS)
                pool.tensor_tensor(nxb[s][:, :, :], window_of_x(w, 0), bn2_rows[:, :, :], ALU.add).then_inc(n_xb[s], 1)
                pool.wait_ge(n_xb[s], i + 1)
                pool.wait_ge(n_h[s], i + 1)
                if not first(turn):
                    pool.wait_ge(n_out[s], i - 1)
                pool.tensor_tensor(nxh[place][:, :, :], nxb[s][:, :, :], nh[place][:, :, :], ALU.add
                                   ).then_inc(n_xh[s], 1)

            split = MORE_FROM * NRING
            run(pool, NW, [(4, split, NRING), (split, 96, NRING)], 0, sum_x)

        @block.scalar
        def _(act):
            def square(i, s):
                act.wait_ge(s_centred[s], i + 1)
                if not first(i):
                    act.wait_ge(s_var[s], i)
                act.activation(squares[s][:, :, :], centred[s][:, :, :], ACT.Square,
                               scale=D ** -0.5).then_inc(s_squared[s], 1)

            def root(i, s):
                act.wait_ge(s_var[s], i + 1)
                act.activation(std[s][:, :], var[s][:, :], ACT.Sqrt, bias=eps[:, 0:1]).then_inc(s_std[s], 1)

            def copy_turned(i, s):
                act.wait_ge(s_turn[s], i + 1)
                if not first(i):
                    act.wait_ge(s_l1[s], i)
                act.copy(turned[s][:, :], bank[s][:, 0:JT * P]).then_inc(s_turned[s], 1)
                act.copy(turned_edge[s][:, :], bank[s][0:D, JT * P:2 * JT * P]).then_inc(s_turned[s], 1)

            def relu(i, s):
                act.wait_ge(s_l1[s], i + 1)
                if not first(i):
                    act.wait_ge(s_l2[s], i)
                for end in (SRC, DST):
                    act.activation(hidden[s][:, end, :], bank[2 + s][:, end * JT * P:(end + 1) * JT * P], ACT.Relu,
                                   bias=b1[:, end:end + 1]).then_inc(s_hidden[s], 1)

            def copy_sums(i, s):
                act.wait_ge(s_joined[s], i + 1)
                if not first(i):
                    act.wait_ge(s_added[s], 16 * KB * i)
                act.copy(to_send[s][:, :, :].rearrange("p k m -> p (k m)"), bank[6 + s][:, :]).then_inc(s_send[s], 1)

            def batch(w):
                w.do(root)
                w.do(relu, -1)
                w.do(square, 1)
                w.do(copy_sums, -2)
                w.do(copy_turned)

            def square_begin(i, s):
                act.wait_ge(b_centred[s], i + 1)
                if not first(i):
                    act.wait_ge(b_var[s], i)
                act.activation(nsquares[s][:, :, :], ncentred[s][:, :, :], ACT.Square,
                               scale=D ** -0.5).then_inc(b_squared[s], 1)

            def root_begin(i, s):
                act.wait_ge(b_var[s], i + 1)
                act.activation(nstd[s][:, :], nvar[s][:, :], ACT.Sqrt, bias=eps[:, 0:1]).then_inc(b_std[s], 1)

            def copy_begin(i, s):
                act.wait_ge(b_turn[s], i + 1)
                if not first(i):
                    act.wait_ge(b_product[s], i)
                act.copy(nturned[s][:, :], bank[s][:, :]).then_inc(b_turned[s], 1)

            def copy_rows(half):
                def copy(i, s):
                    act.wait_ge(b_product[s], i + 1)
                    if not first(i):
                        act.wait_ge(b_stored[s], 16 * i)
                    act.copy(nhidden[s][:, half * 512:(half + 1) * 512], bank[2 + 2 * s + half][:, :]
                             ).then_inc(b_rows[s], 1)
                return copy

            def begin(w):
                w.do(root_begin, 2)
                w.do(square_begin, 3)
                w.do(copy_begin, 1)
                w.do(copy_rows(0), -1)
                w.do(copy_rows(1), -1)

            for k in range(3):
                Step(NW, 0).do(square_begin, k)
                if k < 2:
                    Step(NW, 0).do(root_begin, k)
                if k == 0:
                    copy_begin(0, 0)
            run(act, NW, [(4, 92, 4)], 1, begin)

            act.wait_ge(s_params, 16 * N_PARAMS)
            square(0, 0)
            run(act, NB, [(4, 96, 2)], 2, batch)

            def relu_nodes(i, s):
                act.wait_ge(n_turned[s], 2 * (i + 1))
                if not first(i):
                    act.wait_ge(n_l2[s], i)
                for odd in range(2):
                    act.activation(nhidden[s][:, odd * 512:odd * 512 + 512], bank[2 + 2 * s + odd][:, :], ACT.Relu,
                                   bias=bn1_col[:, 0:1]).then_inc(n_hidden[s], 1)

            run(act, NW, [(4, 96, 4)], 0, lambda w: w.do(relu_nodes))

        @block.tensor
        def _(pe):
            pe.wait_ge(s_const, 6)
            pe.wait_ge(s_rowf, 1)
            for end in (SRC, DST):
                for b in range(2):
                    c = (2 * end + b) * TB
                    last = pe.transpose(bank[6][:, c:c + TB], ends_row[:, end, b, :], ident[0:TB, 0:TB])
            last.then_inc(s_setup_pe, 1)
            pe.wait_ge(s_wn1h, 32)

            def turn_weights():
                pe.wait_ge(s_params, 16 * N_PARAMS)
                for end in (SRC, DST):
                    last = pe.transpose(bank[7][:, end * M:(end + 1) * M], w2[:, end, :], ident[:, :])
                last.then_inc(s_setup_pe, 1)

            def weight_products():
                pe.wait_ge(s_setup_ev, 3)
                pe.wait_ge(s_b2wide, 2)
                for end in (SRC, DST):
                    pe.matmul(bank[6][:, end * M:(end + 1) * M], w2t[:, end, :], wn1_agg[:, :], start=True, stop=True)
                for end in (SRC, DST):
                    last = pe.matmul(bank[6][:, (2 + end) * M:(3 + end) * M], b2_wide[:, end, :], wn1_agg[:, :],
                                     start=True, stop=True)
                last.then_inc(s_setup_pe, 1)

            def turn_begin(i, s, turn, place):
                pe.wait_ge(b_h[s], i + 1)
                if not first(i):
                    pe.wait_ge(b_turned[s], i)
                for q in range(G // 2):
                    last = pe.transpose(bank[s][:, q * P:(q + 1) * P],
                                        nh[place][:, 2 * q:2 * q + 2, :].rearrange("p g d -> p (g d)"), ident[:, :])
                last.then_inc(b_turn[s], 1)

            def product(i, s):
                pe.wait_ge(b_turned[s], i + 1)
                if not first(i):
                    pe.wait_ge(b_rows[s], 2 * i)
                for q in range(G // 2):
                    half, c = divmod(q * 2 * M, 512)
                    last = pe.matmul(bank[2 + 2 * s + half][:, c:c + 2 * M], nturned[s][:, q * P:(q + 1) * P],
                                     wn1_h[:, :, :].rearrange("p a m -> p (a m)"), start=True, stop=True)
                last.then_inc(b_product[s], 1)

            def begin(w):
                w.do(turn_begin, 1, ring=NRING)
                w.do(product)
                if w.least() == 1:
                    turn_weights()
                if w.least() == 3:
                    weight_products()

            turn_begin(0, 0, 0, 0)
            run(pe, NW, [(4, 96, 4)], 0, begin)

            for s in range(2):
                pe.wait_ge(b_rows[s], NW)
                pe.wait_ge(b_turned[s], NW // 2)
            pe.wait_ge(s_setup_ev, 6)

            def turn(i, s):
                if not first(i):
                    pe.wait_ge(s_turned[s], 2 * i)
                if isinstance(i, int) and i == PAIRS - 1 and s == 1:
                    pe.wait_ge(s_edge_in[s], 16 * (i + 2))
                else:
                    pe.wait_ge(s_edge_in[s], 16 * (i + 1))
                pe.wait_ge(s_h[s], i + 1)
                for j in range(JT):
                    pe.transpose(bank[s][:, j * P:(j + 1) * P],
                                 h_ends[s][:, 2 * j:2 * j + 2, :].rearrange("p k d -> p (k d)"), ident[:, :])
                for j in range(JT):
                    last = pe.transpose(bank[s][0:D, (JT + j) * P:(JT + j + 1) * P], edge_in[s][:, j, :], ident[:, :])
                last.then_inc(s_turn[s], 1)

            def layer1(i, s):
                pe.wait_ge(s_turned[s], 2 * (i + 1))
                if not first(i):
                    pe.wait_ge(s_hidden[s], 2 * i)
                for end in (SRC, DST):
                    c = end * JT * P
                    pe.matmul(bank[2 + s][:, c:c + JT * P], w1_ends[:, end, :], turned[s][:, 0:JT * P],
                              start=True, stop=False)
                    last = pe.matmul(bank[2 + s][:, c:c + JT * P], w1_edge[:, end, :], turned_edge[s][:, :],
                                     start=False, stop=True)
                last.then_inc(s_l1[s], 1)

            def layer2(i, s):
                if not first(i):
                    pe.wait_ge(s_message[s], i)
                for end in (SRC, DST):
                    pe.wait_ge(s_hidden[s], 2 * i + 1 + end)
                    for j in range(JT):
                        k = 2 * j + end
                        last = pe.matmul(bank[4 + s][:, k * M:(k + 1) * M], hidden[s][:, end, j * P:(j + 1) * P],
                                         w2n[:, end, :], start=True, stop=True)
                last.then_inc(s_l2[s], 1)

            def join(i, s):
                pe.wait_ge(s_message[s], i + 1)
                pe.wait_ge(s_same[s], i + 1)
                if not first(i):
                    pe.wait_ge(s_send[s], i)
                for k in range(KB):
                    for o in range(k, KB):
                        last = pe.matmul(bank[6 + s][:, k * M:(k + 1) * M], same[s][:, o, k * P:(k + 1) * P],
                                         message[s][:, o, :], start=(o == k), stop=(o == KB - 1))
                last.then_inc(s_joined[s], 1)

            def batch(w):
                w.do(join, -2)
                w.do(turn)
                w.do(layer2, -1)
                w.do(layer1)

            run(pe, NB, [(4, 96, 2)], 2, batch)

            for s in range(2):
                pe.wait_ge(s_send[s], PAIRS)
                pe.wait_ge(s_message[s], PAIRS)

            def turn_table(i, s, turn, place):
                pe.wait_ge(n_tab[place], 16 * (turn + 1))
                if not first(i):
                    pe.wait_ge(n_hidden[s], 2 * i)
                for odd in range(2):
                    for q in range(G // 2):
                        g = 2 * q + odd
                        last = pe.transpose(bank[2 + 2 * s + odd][:, q * P:(q + 1) * P],
                                            ntab[place][:, g * M:(g + 1) * M], ident[:, :])
                    last.then_inc(n_turned[s], 1)

            def layer2_nodes(i, s):
                if not first(i):
                    pe.wait_ge(n_out[s], i)
                pe.wait_ge(n_hidden[s], 2 * (i + 1))
                for odd in range(2):
                    for q in range(G // 2):
                        g, c = 2 * q + odd, (odd * (G // 2) + q) * P
                        last = pe.matmul(bank[6 + s][:, g * D:(g + 1) * D], nhidden[s][:, c:c + P], wn2[:, :],
                                         start=True, stop=True)
                last.then_inc(n_l2[s], 1)

            def window(w):
                w.do(turn_table, ring=NRING)
                w.do(layer2_nodes, -1)

            run(pe, NW, [(4, 96, 4)], 1, window)

        @block.vector
        def _(dve):
            dve.memset(eps[:, :], EPS).then_inc(s_const, 1)
            dve.memset(wn1_h[0:D, 1, :], 0.0).then_inc(s_const, 1)
            dve.memset(wn1_h[D:2 * D, 0, :], 0.0).then_inc(s_const, 1)

            def edge_columns():
                dve.memset(zeros[:, :], 0.0).then_inc(s_zeros, 1)
                dve.wait_ge(s_ends, 6 * 16)
                dve.tensor_copy(ends_row[:, :, :, :], ends_int[:, :, :, :]).then_inc(s_rowf, 1)
                dve.wait_ge(s_setup_pe, 1)
                for end in (SRC, DST):
                    dve.tensor_copy(ends_col[:, :, end], bank[6][:, 2 * end * TB:(2 * end + 2) * TB]
                                    ).then_inc(s_setup_ev, 1)
                dve.wait_ge(s_setup_ev, 2)
                dve.tensor_scalar(gather_first[:, :], ends[:, 0:NB * KB], float(N - 1), None, ALU.min
                                  ).then_inc(s_first, 1)

            def copy_turned_weights():
                dve.wait_ge(s_params, 16 * N_PARAMS)
                for end in (SRC, DST):
                    dve.tensor_copy(b2_wide[:, end, :], b2[:, end:end + 1].to_broadcast([P, P])).then_inc(s_b2wide, 1)
                dve.wait_ge(s_setup_pe, 2)
                dve.tensor_copy(w2t[:, :, :].rearrange("p a m -> p (a m)"), bank[7][:, 0:2 * M]).then_inc(s_setup_ev, 1)

            def copy_weight_products():
                dve.wait_ge(s_setup_pe, 3)
                dve.tensor_copy(w2n[:, :, :].rearrange("p a m -> p (a m)"), bank[6][:, 0:2 * M]).then_inc(s_setup_ev, 1)
                for j in range(JT):
                    dve.tensor_copy(b2n[:, 2 * j:2 * j + 2, :].rearrange("p a m -> p (a m)"),
                                    bank[6][:, 2 * M:4 * M]).then_inc(s_setup_ev, 1)

            ends = ends_col[:, :, :].rearrange("p t e -> p (t e)")

            def gather_rows(w):
                place = w.of(2 * RING, 2 * RING)[1] // 2
                dve.tensor_copy(gather_at[place][:, :], gather_first[:, bass.ds(w.number(2 * RING + 1) * KB, KB)]
                                ).then_inc(s_gat[place], 1)

            def centre(w, k):
                i, s = w.of(2, k)
                if s == 0:
                    rows = got_even[:, bass.ds(i, 1), :]
                else:
                    turn, place = w.of(2 * RING, k)
                    rows = got_odd[place // 2][:, :, :]
                    dve.wait_ge(s_got[place // 2], 16 * KB * (turn + 1))
                rows = rows.rearrange("p a (k d) -> p (a k) d", d=D)
                if not first(i):
                    dve.wait_ge(s_h[s], i)
                dve.tensor_reduce(sums[s][:, :], rows, AX.X, ALU.add).then_inc(s_sums[s], 1)
                dve.wait_ge(s_sums[s], i + 1)
                dve.scalar_tensor_tensor(out=centred[s][:, :, :], in0=sums[s][:, :].to_broadcast([P, KB, D]),
                                         scalar=-1.0 / D, in1=rows, op0=ALU.mult, op1=ALU.add
                                         ).then_inc(s_centred[s], 1)

            def match(i, s):
                if not first(i):
                    dve.wait_ge(s_sat[s], i)
                dve.tensor_copy(ids[s][:, :], ends[:, bass.ds((2 * i + s) * KB, KB)]).then_inc(s_ids[s], 1)
                dve.wait_ge(s_ids[s], i + 1)
                dve.wait_ge(s_others[s], 32 * (i + 1))
                if not first(i):
                    dve.wait_ge(s_joined[s], i)
                row = others[s][:, :, :, :].rearrange("p j e q -> p (j e q)")
                for o in range(KB):
                    w = (o + 1) * P
                    last = dve.tensor_scalar(same[s][:, o, 0:w], row[:, 0:w], ids[s][:, o:o + 1], None, ALU.is_equal)
                last.then_inc(s_same[s], 1)

            def variance(i, s):
                dve.wait_ge(s_squared[s], i + 1)
                dve.tensor_reduce(var[s][:, :], squares[s][:, :, :], AX.X, ALU.add).then_inc(s_var[s], 1)

            def targets(i, s):
                dve.wait_ge(s_same[s], i + 1)
                for k in range(KB):
                    w = (k + 1) * P
                    last = dve.tensor_tensor_reduce(junk[s][:, k, 0:w], same[s][:, k, 0:w], earlier[:, KB * P - w:],
                                                    1.0, 0.0, ALU.mult, ALU.add, before[s][:, k:k + 1])
                last.then_inc(s_before[s], 1)
                dve.tensor_tensor(to_spare[s][:, :], spare[:, :], ids[s][:, :], ALU.subtract).then_inc(s_tospare[s], 1)
                dve.wait_ge(s_before[s], i + 1)
                dve.wait_ge(s_tospare[s], i + 1)
                dve.scalar_tensor_tensor(out=moved[s][:, :], in0=before[s][:, :], scalar=1.0, in1=to_spare[s][:, :],
                                         op0=ALU.min, op1=ALU.mult).then_inc(s_moved[s], 1)

            def aim(i, s):
                dve.wait_ge(s_moved[s], i + 1)
                if not first(i):
                    dve.wait_ge(s_added[s], 16 * KB * i)
                dve.tensor_tensor(scatter_at[s][:, :], moved[s][:, :], ids[s][:, :], ALU.add).then_inc(s_sat[s], 1)

            def messages(i, s):
                dve.wait_ge(s_l2[s], i + 1)
                if not first(i):
                    dve.wait_ge(s_joined[s], i)
                dve.tensor_tensor(message[s][:, :, :].rearrange("p k m -> p (k m)"), bank[4 + s][:, :],
                                  b2n[:, :, :].rearrange("p k m -> p (k m)"), ALU.add).then_inc(s_message[s], 1)

            def normal(i, s):
                dve.wait_ge(s_std[s], i + 1)
                dve.reciprocal(rstd[s][:, :], std[s][:, :]).then_inc(s_rstd[s], 1)
                dve.wait_ge(s_rstd[s], i + 1)
                if not first(i):
                    dve.wait_ge(s_turn[s], i)
                dve.scalar_tensor_tensor(out=h_ends[s][:, :, :], in0=centred[s][:, :, :], scalar=0.0,
                                         in1=rstd[s][:, :].to_broadcast([P, KB, D]), op0=ALU.max, op1=ALU.mult
                                         ).then_inc(s_h[s], 1)

            def batch(w):
                w.do(variance)
                w.do(aim, -2)
                if w.there(1):
                    centre(w, 1)
                w.do(match, -1)
                w.do(normal)
                if w.n % 2 == 0 and w.there(2 * RING):
                    gather_rows(w)
                w.do(targets, -1)
                w.do(messages, -1)

            def of_window(a, i, s):
                return a[:, bass.ds(2 * i + s, 1), :].rearrange("p a g -> p (a g)")

            def sum_begin(i, s, turn, place):
                dve.wait_ge(b_x[place], 16 * (turn + 1))
                dve.tensor_reduce(of_window(all_sums, i, s), nx[place][:, :, :], AX.X, ALU.add).then_inc(b_sums[s], 1)

            def centre_begin(i, s, turn, place):
                dve.wait_ge(b_sums[s], i + 1)
                if not first(i):
                    dve.wait_ge(b_h[s], i)
                of_all = of_window(all_sums, i, s)
                dve.scalar_tensor_tensor(out=ncentred[s][:, :, :], in0=of_all.to_broadcast([P, G, D]),
                                         scalar=-1.0 / D, in1=nx[place][:, :, :], op0=ALU.mult, op1=ALU.add
                                         ).then_inc(b_centred[s], 1)

            def variance_begin(i, s):
                dve.wait_ge(b_squared[s], i + 1)
                dve.tensor_reduce(nvar[s][:, :], nsquares[s][:, :, :], AX.X, ALU.add).then_inc(b_var[s], 1)

            def invert_begin(i, s):
                dve.wait_ge(b_std[s], i + 1)
                dve.reciprocal(of_window(all_rstd, i, s), nstd[s][:, :]).then_inc(b_rstd[s], 1)

            def normal_begin(i, s, turn, place):
                dve.wait_ge(b_rstd[s], i + 1)
                of_all = of_window(all_rstd, i, s)
                if not first(turn):
                    dve.wait_ge(b_turn[s], i - 1)
                dve.scalar_tensor_tensor(out=nh[place][:, :, :], in0=ncentred[s][:, :, :], scalar=0.0,
                                         in1=of_all.to_broadcast([P, G, D]), op0=ALU.max, op1=ALU.mult
                                         ).then_inc(b_h[s], 1)

            def begin(w):
                w.do(sum_begin, 3, ring=NRING)
                w.do(variance_begin, 2)
                w.do(centre_begin, 3, ring=NRING)
                w.do(invert_begin, 2)
                w.do(normal_begin, 2, ring=NRING)
                if w.least() == 2:
                    copy_turned_weights()
                if w.least() == 92:
                    copy_weight_products()

            for k in range(3):
                if k == 1:
                    edge_columns()
                Step(NW, 0).do(sum_begin, k, ring=NRING)
                Step(NW, 0).do(centre_begin, k, ring=NRING)
                if k < 2:
                    Step(NW, 0).do(variance_begin, k)
                    Step(NW, 0).do(invert_begin, k)
                    Step(NW, 0).do(normal_begin, k, ring=NRING)
            run(dve, NW, [(4, 92, 4)], 0, begin)

            dve.wait_ge(s_setup_ev, 6)
            dve.wait_ge(s_const, 6)
            dve.wait_ge(s_got_even, 16 * KB * PAIRS)
            centre(Step(NB, 0), 0)
            run(dve, NB, [(8, 88, 2 * RING)], 2, batch)

            def centre_nodes(w, k):
                if not w.there(k):
                    return
                i, s = w.of(2, k)
                wait_for_x(dve, w, k)
                if not first(i):
                    dve.wait_ge(n_h[s], i)
                dve.scalar_tensor_tensor(out=ncentred[s][:, :, :],
                                         in0=all_sums[:, bass.ds(2 * i + s, 1), :].rearrange("p a g -> p (a g)")
                                         .to_broadcast([P, G, D]),
                                         scalar=-1.0 / D, in1=window_of_x(w, k), op0=ALU.mult, op1=ALU.add
                                         ).then_inc(n_centred[s], 1)

            def normal_nodes(i, s, turn, place):
                dve.wait_ge(n_centred[s], i + 1)
                if not first(turn):
                    dve.wait_ge(n_xh[s], i - 1)
                dve.scalar_tensor_tensor(out=nh[place][:, :, :], in0=ncentred[s][:, :, :], scalar=0.0,
                                         in1=all_rstd[:, bass.ds(2 * i + s, 1), :].rearrange("p a g -> p (a g)")
                                         .to_broadcast([P, G, D]), op0=ALU.max, op1=ALU.mult).then_inc(n_h[s], 1)

            def output(i, s, turn, place):
                dve.wait_ge(n_l2[s], i + 1)
                dve.wait_ge(n_xh[s], i + 1)
                if not first(i):
                    dve.wait_ge(n_stored[s], 16 * i)
                dve.tensor_tensor(nout[s][:, :, :].rearrange("p g d -> p (g d)"), bank[6 + s][:, :],
                                  nxh[place][:, :, :].rearrange("p g d -> p (g d)"), ALU.add).then_inc(n_out[s], 1)

            def window(w):
                centre_nodes(w, 3)
                w.do(normal_nodes, 2, ring=NRING)
                w.do(output, -1, ring=NRING)

            for k in range(3):
                centre_nodes(Step(NW, 0), k)
                if k < 2:
                    Step(NW, 0).do(normal_nodes, k, ring=NRING)
            split = (MORE_FROM - 1) * NRING
            run(dve, NW, [(4, split, NRING), (split, 92, NRING)], 1, window)


_INS = ['x', 'src', 'dst', 'edge_attr_64', 'L0_gnn_W1_f', 'L0_gnn_b1_f', 'L0_gnn_W2_f', 'L0_gnn_b2_f',
        'L0_gnn_W1_r', 'L0_gnn_b1_r', 'L0_gnn_W2_r', 'L0_gnn_b2_r', 'L0_gnn_Wn1', 'L0_gnn_bn1', 'L0_gnn_Wn2',
        'L0_gnn_bn2']


def kernel(**inputs):
    import numpy as _np
    import concourse.bacc as _bacc
    from concourse import mybir as _mybir
    from concourse.bass_utils import run_bass_kernel_spmd as _run

    nc = _bacc.Bacc("TRN2", target_bir_lowering=False, num_devices=1)
    arrays, args = {}, []
    for name in _INS:
        a = _np.ascontiguousarray(inputs[name])
        arrays[f"in_{name}"] = a
        args.append(nc.dram_tensor(f"in_{name}", a.shape, _mybir.dt.from_np(a.dtype), kind="ExternalInput").ap())
    out = nc.dram_tensor("out_x", inputs["x"].shape, _mybir.dt.float32, kind="ExternalOutput").ap()
    gnn_layer(nc, *args, out)
    r = _run(nc, [arrays], core_ids=[0])
    return r.results[0]["out_x"]
```
